# Optimizing a Trainium2 kernel written in Bass

```python
import numpy as np
import jax
import jax.numpy as jnp

def _softmax(x, axis=-1):
    return jax.nn.softmax(x, axis=axis)

def _gelu(x):
    return jax.nn.gelu(x, approximate=True)

def _silu(x):
    return jax.nn.silu(x)

def _sigmoid(x):
    return jax.nn.sigmoid(x)

def _layernorm(x, axis=-1, eps=1e-05):
    m = jnp.mean(x, axis=axis, keepdims=True)
    v = jnp.var(x, axis=axis, keepdims=True)
    return (x - m) / jnp.sqrt(v + eps)

def _scatter_add(tgt, idx, src, axis=0):
    return tgt.at[idx].add(src)

def _segment_sum(src, seg, n):
    return jax.ops.segment_sum(src, seg, n)
kernel_name = 'mk_seq_postln_d1_jaxref_r8_846206'

def setup_inputs(seed: int=0):
    np.random.seed(seed)
    _w = jnp.asarray

    def _L0_attn_setup():
        import jax, jax.numpy as jnp
        import numpy as np
        D_MODEL = 256
        N_HEADS = 16
        D_HEAD = D_MODEL // N_HEADS
        B, S = (2, 256)
        EPS = 1e-05

        def _mhsa(X, ln_g, ln_b, Wq, bq, Wk, bk, Wv, bv, Wo, bo):
            n_ctx = X.shape[-2]
            mu = jnp.mean(X, axis=-1, keepdims=True)
            var = jnp.mean(jnp.square(X - mu), axis=-1, keepdims=True)
            Xn = (X - mu) * jax.lax.rsqrt(var + EPS) * ln_g + ln_b

            def split_heads(t):
                return t.reshape(t.shape[:-1] + (N_HEADS, D_HEAD)).swapaxes(-2, -3)
            Q = split_heads(Xn @ Wq + bq)
            K = split_heads(Xn @ Wk + bk)
            V = split_heads(Xn @ Wv + bv)
            scores = jnp.einsum('bhqd,bhkd->bhqk', Q, K) / jnp.sqrt(jnp.float32(D_HEAD))
            causal = jnp.tril(jnp.ones((n_ctx, n_ctx), dtype=bool))
            scores = jnp.where(causal, scores, jnp.float32(-jnp.inf))
            A = jax.nn.softmax(scores, axis=-1)
            AV = jnp.einsum('bhqk,bhkd->bhqd', A, V)
            AV = AV.swapaxes(-2, -3).reshape(X.shape[:-1] + (D_MODEL,))
            return AV @ Wo + bo
        key = jax.random.key(seed)
        ks = jax.random.split(key, 10)
        sd = 1.0 / np.sqrt(D_MODEL)
        inp = {'X': jax.random.normal(ks[0], (B, S, D_MODEL), dtype=jnp.float32), 'ln_g': jnp.ones((D_MODEL,), jnp.float32), 'ln_b': jnp.zeros((D_MODEL,), jnp.float32), 'Wq': jax.random.uniform(ks[1], (D_MODEL, D_MODEL), jnp.float32, -sd, sd), 'bq': jax.random.uniform(ks[2], (D_MODEL,), jnp.float32, -sd, sd), 'Wk': jax.random.uniform(ks[3], (D_MODEL, D_MODEL), jnp.float32, -sd, sd), 'bk': jax.random.uniform(ks[4], (D_MODEL,), jnp.float32, -sd, sd), 'Wv': jax.random.uniform(ks[5], (D_MODEL, D_MODEL), jnp.float32, -sd, sd), 'bv': jax.random.uniform(ks[6], (D_MODEL,), jnp.float32, -sd, sd), 'Wo': jax.random.uniform(ks[7], (D_MODEL, D_MODEL), jnp.float32, -sd, sd), 'bo': jax.random.uniform(ks[8], (D_MODEL,), jnp.float32, -sd, sd)}
        return inp
    _L0_attn_in = _L0_attn_setup()

    def _L0_ffn_setup():
        import jax, jax.numpy as jnp
        import numpy as np
        B, S, D, K, R = (4, 256, 256, 8, 64)
        key = jax.random.key(seed)
        ks = jax.random.split(key, 7)
        x = jax.random.normal(ks[0], (B, S, D), dtype=jnp.float32)
        U = jax.random.normal(ks[1], (K, D, R), dtype=jnp.float32) * 0.02
        V = jax.random.normal(ks[2], (K, R, D), dtype=jnp.float32) * 0.02
        W1 = jax.random.normal(ks[3], (D, D), dtype=jnp.float32) * 0.02
        b1 = jnp.zeros((D,), dtype=jnp.float32)
        W2 = jax.random.normal(ks[4], (D, K), dtype=jnp.float32) * 0.02
        b2 = jnp.zeros((K,), dtype=jnp.float32)
        return {'x': x, 'U': U, 'V': V, 'W1': W1, 'b1': b1, 'W2': W2, 'b2': b2}
    _L0_ffn_in = _L0_ffn_setup()
    _d = {'L0_attn_X': _L0_attn_in['X'], 'L0_attn_ln_g': _L0_attn_in['ln_g'], 'L0_attn_ln_b': _L0_attn_in['ln_b'], 'L0_attn_Wq': _L0_attn_in['Wq'], 'L0_attn_bq': _L0_attn_in['bq'], 'L0_attn_Wk': _L0_attn_in['Wk'], 'L0_attn_bk': _L0_attn_in['bk'], 'L0_attn_Wv': _L0_attn_in['Wv'], 'L0_attn_bv': _L0_attn_in['bv'], 'L0_attn_Wo': _L0_attn_in['Wo'], 'L0_attn_bo': _L0_attn_in['bo'], 'L0_ffn_U': _L0_ffn_in['U'], 'L0_ffn_V': _L0_ffn_in['V'], 'L0_ffn_W1': _L0_ffn_in['W1'], 'L0_ffn_b1': _L0_ffn_in['b1'], 'L0_ffn_W2': _L0_ffn_in['W2'], 'L0_ffn_b2': _L0_ffn_in['b2']}
    _x0 = _d['L0_attn_X']
    _d['L0_attn_X'] = jax.random.normal(jax.random.fold_in(jax.random.key(seed), 1), (2, 1024, 256), dtype=_x0.dtype)
    del _x0
    return _d

def reference(L0_attn_X, L0_attn_ln_g, L0_attn_ln_b, L0_attn_Wq, L0_attn_bq, L0_attn_Wk, L0_attn_bk, L0_attn_Wv, L0_attn_bv, L0_attn_Wo, L0_attn_bo, L0_ffn_U, L0_ffn_V, L0_ffn_W1, L0_ffn_b1, L0_ffn_W2, L0_ffn_b2):

    def _L0_attn_ref(X, ln_g, ln_b, Wq, bq, Wk, bk, Wv, bv, Wo, bo):
        import jax, jax.numpy as jnp
        import numpy as np
        D_MODEL = 256
        N_HEADS = 16
        D_HEAD = D_MODEL // N_HEADS
        B, S = (2, 256)
        EPS = 1e-05

        def _mhsa(X, ln_g, ln_b, Wq, bq, Wk, bk, Wv, bv, Wo, bo):
            n_ctx = X.shape[-2]
            mu = jnp.mean(X, axis=-1, keepdims=True)
            var = jnp.mean(jnp.square(X - mu), axis=-1, keepdims=True)
            Xn = (X - mu) * jax.lax.rsqrt(var + EPS) * ln_g + ln_b

            def split_heads(t):
                return t.reshape(t.shape[:-1] + (N_HEADS, D_HEAD)).swapaxes(-2, -3)
            Q = split_heads(Xn @ Wq + bq)
            K = split_heads(Xn @ Wk + bk)
            V = split_heads(Xn @ Wv + bv)
            scores = jnp.einsum('bhqd,bhkd->bhqk', Q, K) / jnp.sqrt(jnp.float32(D_HEAD))
            causal = jnp.tril(jnp.ones((n_ctx, n_ctx), dtype=bool))
            scores = jnp.where(causal, scores, jnp.float32(-jnp.inf))
            A = jax.nn.softmax(scores, axis=-1)
            AV = jnp.einsum('bhqk,bhkd->bhqd', A, V)
            AV = AV.swapaxes(-2, -3).reshape(X.shape[:-1] + (D_MODEL,))
            return AV @ Wo + bo
        return _mhsa(X, ln_g, ln_b, Wq, bq, Wk, bk, Wv, bv, Wo, bo)

    def _L0_ffn_ref(x, U, V, W1, b1, W2, b2):
        import jax, jax.numpy as jnp
        import numpy as np
        B, S, D, K, R = (4, 256, 256, 8, 64)
        h = jax.nn.relu(jnp.einsum('bsd,de->bse', x, W1) + b1)
        alpha = jax.nn.softmax(jnp.einsum('bse,ek->bsk', h, W2) + b2, axis=-1)
        vx = jnp.einsum('krd,bsd->bskr', V, x)
        uvx = jnp.einsum('kdr,bskr->bskd', U, vx)
        out = jnp.einsum('bsk,bskd->bsd', alpha, uvx)
        return out
    x = L0_attn_X
    x = _layernorm(x + _L0_attn_ref(x, L0_attn_ln_g, L0_attn_ln_b, L0_attn_Wq, L0_attn_bq, L0_attn_Wk, L0_attn_bk, L0_attn_Wv, L0_attn_bv, L0_attn_Wo, L0_attn_bo), axis=-1)
    x = _layernorm(x + _L0_ffn_ref(x, L0_ffn_U, L0_ffn_V, L0_ffn_W1, L0_ffn_b1, L0_ffn_W2, L0_ffn_b2), axis=-1)
    return x

_drawn_inputs = setup_inputs


def setup_inputs(seed=0):
    import zlib

    import numpy as np

    out = dict(_drawn_inputs(seed))
    spreads = {'L0_attn_ln_g': (1.0, 0.6),
     'L0_attn_ln_b': (0.0, 0.1),
     'L0_ffn_b1': (0.0, 0.8),
     'L0_ffn_b2': (0.0, 0.8)}
    factors = {'L0_attn_Wq': 4.252,
     'L0_attn_bq': 8.0,
     'L0_attn_Wk': 4.257,
     'L0_attn_bk': 64.0,
     'L0_ffn_U': 3.13,
     'L0_ffn_V': 3.131,
     'L0_ffn_W1': 8.0,
     'L0_ffn_W2': 8.0,
     'L0_attn_bv': 2.737}
    for name, (base, spread) in spreads.items():
        noise = np.random.default_rng([zlib.crc32(name.encode()), seed]).standard_normal(out[name].shape)
        drawn = base * np.exp(spread * noise) if base else spread * noise
        out[name] = jnp.asarray(drawn.astype(out[name].dtype))
    for name, factor in factors.items():
        out[name] = (out[name] * factor).astype(out[name].dtype)
    return out
```

```python
from contextlib import ExitStack

import concourse.bass as bass
from concourse import mybir

ALU = mybir.AluOpType
ACT = mybir.ActivationFunctionType
AX = mybir.AxisListType
F32 = mybir.dt.float32
F32R = mybir.dt.float32r
BF16 = mybir.dt.bfloat16
I32 = mybir.dt.int32

P = 128
HEADS = 16
DH = 16
HPG = 4
VW = 32
CHUNK = 512
LN_EPS = 1e-5
MASKED = -1e30
RSQRT_MAGIC = float(0x5F3759DF)
KROWS = 3 * DH + 2
MAX_LEAD = 6


def attention_plan(groups, tiles):
    units, steps = max_units(tiles), score_steps(tiles)
    n_max, n_steps = len(units) * groups, len(steps) * groups
    plan, issued, rows_due = [], 0, []

    def issue_max(upto, k):
        nonlocal issued
        while issued < min(upto, n_max):
            g, u = divmod(issued, len(units))
            plan.append(("max", g, u))
            issued += 1
            if u == len(units) - 1:
                rows_due.append((issued + 2, g))
            while rows_due and (issued >= rows_due[0][0]):
                plan.append(("rows", rows_due.pop(0)[1]))

    issue_max(len(units) + MAX_LEAD, -1)
    per_step = len(units) / len(steps)
    for k in range(n_steps + 1):
        g, s = divmod(k, len(steps))
        upto = len(units) + MAX_LEAD + int((k + 1) * per_step)
        if k < n_steps:
            plan += [("score", g, s, 0), ("score", g, s, 1)]
        if k >= 2:
            pg, ps = divmod(k - 2, len(steps))
            if steps[ps][3]:
                plan.append(("drain", pg, steps[ps][0]))
        issue_max(upto - 1, k)
        if k < n_steps:
            plan += [("score", g, s, 2), ("score", g, s, 3)]
        if k >= 1:
            plan.append(("value", *divmod(k - 1, len(steps))))
        issue_max(upto, k)
        if k >= 2 and steps[(k - 2) % len(steps)][3]:
            plan.append(("turn", (k - 2) // len(steps), steps[(k - 2) % len(steps)][0]))
        if issued == n_max and rows_due:
            plan.append(("rows", rows_due.pop(0)[1]))
    plan += [("drain", groups - 1, steps[-1][0]), ("turn", groups - 1, steps[-1][0])]
    return plan


def max_units(tiles):
    units = []
    for t in range(tiles):
        w = (t + 1) * P
        n = 4 if w <= 256 else 2 if w <= CHUNK else 1
        units += [(t, list(range(j, j + n)), w) for j in range(0, HPG, n)]
    return units


def score_steps(tiles):
    per = CHUNK // P
    return [(c, kt, max(kt * P, c * CHUNK), kt == per * c + per - 1)
            for c in range(tiles // per) for kt in range(per * (c + 1))]


def block_kernel(nc, x, vecs, rows, wq, wk, wv, wo, w1, w2, vt, ut, out):
    NB, S, D = x.shape
    T = S // P
    C = S // CHUNK
    TPC = CHUNK // P
    KC = D // P
    E = w2.shape[1]
    ER = vt.shape[1]
    RC = ER // P
    G = HEADS // HPG
    PAIRS = HPG // 2
    units, steps = max_units(T), score_steps(T)
    U, ST = len(units), len(steps)
    plan = attention_plan(G, T)

    x_v = x.rearrange("b (t p) d -> b p t d", p=P)
    out_v = out.rearrange("b (t p) d -> b p t d", p=P)

    with ExitStack() as ctx:
        def sb(name, shape, dt=F32):
            return ctx.enter_context(nc.sbuf_tensor(name, shape, dt))

        def sem(name):
            return ctx.enter_context(nc.semaphore(name))

        w_qk = sb("w_qk", [P, KC, 2, D])
        w_v = sb("w_v", [P, KC, D])
        w_o = sb("w_o", [P, KC, D])
        w_1 = sb("w_1", [P, KC, D])
        w_2 = sb("w_2", [P, KC, E])
        v_t = sb("v_t", [P, KC, ER])
        u_t = sb("u_t", [P, RC, D])
        cols = sb("cols", [P, 5, KC])
        flat = sb("flat", [P, 2 * D + E])
        ident = sb("ident", [P, P])
        ident_b = sb("ident_b", [P, P], BF16)
        mask = sb("mask", [P, P], BF16)

        x_in = sb("x_in", [P, T, D])
        x_bo = sb("x_bo", [P, T, D])
        xh = sb("xh", [P, T, D])
        xt = sb("xt", [P, C, KC, CHUNK])
        qk = sb("qk", [P, KC, 2, 2, S])
        va = sb("va", [P, T, HEADS, VW])
        stq = [sb(f"stq{i}", [P, PAIRS, S], F32R) for i in range(3)]
        stk = [sb(f"stk{i}", [P, PAIRS, S], F32R) for i in range(3)]
        pr = [sb(f"pr{i}", [P, HPG, CHUNK]) for i in range(3)]
        mx = sb("mx", [P, 2, HPG * T])
        mhl = sb("mhl", [P, 2, HPG * T], F32R)
        mrow = sb("mrow", [2 * HPG * T, P], F32R)
        av_raw = sb("av_raw", [P, 2, CHUNK])
        rs = sb("rs", [P, TPC, HPG])
        o_sb = sb("o_sb", [P, T, D])
        st6 = sb("st6", [P, T, 6])
        mv = sb("mv", [P, T, 2])
        nv = sb("nv", [P, 4, TPC])
        rstd = sb("rstd", [P, T])
        lg = sb("lg", [P, C, TPC, E])
        le = sb("le", [P, C, TPC, E])
        sm = sb("sm", [P, C, TPC])
        alpha = sb("alpha", [P, C, TPC, E])

        qk_flat = qk[:].rearrange("p a b c s -> p (a b c s)")

        def reuse(i):
            return qk_flat[:, i * KC * S:(i + 1) * KC * S]

        o_t = reuse(0).rearrange("p (k s) -> p k s", k=KC)
        x1_t = reuse(1).rearrange("p (k s) -> p k s", k=KC)
        h_t = reuse(2).rearrange("p (k s) -> p k s", k=KC)
        r2 = reuse(3).rearrange("p (t d) -> p t d", t=T)
        y = pr[0][:].rearrange("p h (t d) -> p (h t) d", d=D)
        r1 = pr[1][:].rearrange("p h (t d) -> p (h t) d", d=D)
        avx = pr[2][:, 0:2, :]
        avt = pr[2][:, 2:4, :]
        x1 = xh

        ps = ctx.enter_context(nc.psum_tensor("ps", [P, 8, CHUNK], F32))

        s_w = sem("s_w")
        s_x = [sem(f"s_x{i}") for i in range(4)]
        s_const = sem("s_const")
        s_xbo = sem("s_xbo")
        s_dve = sem("s_dve")
        s_xh = sem("s_xh")
        s_ra = sem("s_ra")
        s_ra_free = sem("s_ra_free")
        s_rd = sem("s_rd")
        s_rd_free = sem("s_rd_free")
        s_high = sem("s_high")
        s_va = sem("s_va")
        s_stack = [sem(f"s_stack{g}") for g in range(G)]
        s_max = sem("s_max")
        s_maxed = sem("s_maxed")
        s_mhl = sem("s_mhl")
        s_misc = sem("s_misc")
        s_misc_free = sem("s_misc_free")
        s_mrow = sem("s_mrow")
        s_score = sem("s_score")
        s_exp = sem("s_exp")
        s_causal = sem("s_causal")
        s_value = sem("s_value")
        s_drain = sem("s_drain")
        s_o = sem("s_o")
        s_x1 = sem("s_x1_made")
        s_r1 = sem("s_r1")
        s_lg = sem("s_lg")
        s_le = sem("s_le")
        s_avx = sem("s_avx")
        s_y = sem("s_y")
        s_out = sem("s_out")

        ring_a = ([("xt", c, k) for c in range(C) for k in range(KC)],
                  [("ot", c, k) for c in range(C) for k in range(KC)]
                  + [(n, c, k) for c in range(C) for n in ("x1t", "h") for k in range(KC)]
                  + [("avt", t) for t in range(T)])
        ffn = []
        for i in range(T + 2):
            ffn += [("vx", i)] * (i < T) + [("avt", i - 1)] * (1 <= i <= T) + [("u", i - 2)] * (i >= 2)
        project = [("qk", m, c, w) for m in range(KC) for c in range(C) for w in range(2)]
        ring_d = (project + [("v", t) for t in range(0, T, 2)],
                  [("r1", t) for t in range(0, T, 2)] + [("lg", c) for c in range(C)]
                  + [f for f in ffn if f[0] != "avt"])
        in_a = {k: i for i, k in enumerate(ring_a[0] + ring_a[1])}
        in_d = {k: i for i, k in enumerate(ring_d[0] + ring_d[1])}
        A, AD = len(in_a), len(in_d)

        def bank_a(k):
            return ps[:, in_a[k] % 4, :]

        def bank_d(k):
            return ps[:, 4 + in_d[k] % 4, :]

        def max_bank(g, u):
            return ps[:, 2 * ((g * U + u) % 2):2 * ((g * U + u) % 2) + 2, :]

        def n_unit(g, u):
            return g * U + u + 1

        def n_step(g, s):
            return g * ST + s + 1

        diagonal = [s for s, (c, kt, q0, _) in enumerate(steps) if q0 == kt * P]
        misc = [ev for ev in plan if ev[0] in ("rows", "turn")]
        n_misc = {ev: i + 1 for i, ev in enumerate(misc)}
        MISC = len(misc)
        block = ctx.enter_context(nc.Block())

        @block.sync
        def _(sp):
            def move_rows(sp, b, g):
                sp.wait_ge(s_misc_free, b * MISC + n_misc[("rows", g)])
                n = PAIRS * T
                for part in range(2):
                    for half in range(2):
                        row = 64 * half + 3 * DH + part
                        i = (2 * part + half) * n
                        dst = stq[g % 3][row:row + 1, :, :].rearrange("p a (t n) -> p (a t) n", t=T)
                        sp.dma_start(dst.bitcast(F32), mrow[i:i + n, :].bitcast(F32)).then_inc(s_mrow, 16)

            for i in range(4):
                sp.dma_start(x_in[:, 2 * i:2 * i + 2, :], x_v[0, :, 2 * i:2 * i + 2, :]).then_inc(s_x[i], 16)
                if i == 0:
                    sp.dma_start(cols[:], vecs.rearrange("p (v k) -> p v k", v=5)).then_inc(s_w, 16)
                    sp.dma_start(flat[:], rows.partition_broadcast(P)).then_inc(s_w, 16)
            sp.dma_start(w_qk[:, :, 0, :], wq.rearrange("(k p) n -> p k n", p=P)).then_inc(s_w, 16)
            sp.dma_start(w_qk[:, :, 1, :], wk.rearrange("(k p) n -> p k n", p=P)).then_inc(s_w, 16)
            sp.dma_start(w_v[:], wv.rearrange("(k p) n -> p k n", p=P)).then_inc(s_w, 16)
            sp.dma_start(w_o[:], wo.rearrange("(k p) n -> p k n", p=P)).then_inc(s_w, 16)
            sp.dma_start(w_1[:], w1.rearrange("(k p) n -> p k n", p=P)).then_inc(s_w, 16)
            sp.dma_start(w_2[:], w2.rearrange("(k p) n -> p k n", p=P)).then_inc(s_w, 16)
            sp.dma_start(v_t[:], vt.rearrange("(k p) n -> p k n", p=P)).then_inc(s_w, 16)
            sp.dma_start(u_t[:], ut.rearrange("(k p) n -> p k n", p=P)).then_inc(s_w, 16)
            for b in range(NB):
                if b:
                    for i in range(4):
                        sp.dma_start(x_in[:, 2 * i:2 * i + 2, :], x_v[b, :, 2 * i:2 * i + 2, :]).then_inc(s_x[i], 16)
                for g in range(G):
                    if g % 2 == 0:
                        sp.wait_ge(s_rd_free, b * AD + 2 * C * (g // 2 + 1))
                    if g >= 3:
                        sp.wait_ge(s_value, b * G * ST + n_step(g - 3, ST - 1))
                    if b == 0 and g == 0:
                        sp.wait_ge(s_const, 5)
                    m, base = g // 2, (g % 2) * HPG * DH
                    for j in range(HPG):
                        src = slice(base + j * DH, base + (j + 1) * DH)
                        for w, stack, parts in ((0, stq[g % 3], (0, 0, 1)), (1, stk[g % 3], (0, 1, 0))):
                            for r, part in enumerate(parts):
                                dst = 64 * (j % 2) + r * DH
                                sp.dma_start(stack[dst:dst + DH, j // 2, :].bitcast(F32),
                                             qk[src, m, w, part, :]).then_inc(s_stack[g], 16)
                    if g == 2:
                        move_rows(sp, b, 0)
                        move_rows(sp, b, 1)
                move_rows(sp, b, 2)
                move_rows(sp, b, 3)
                for i in range(T // 2):
                    sp.wait_ge(s_y, b * T + 2 * i + 2)
                    sp.dma_start(out_v[b, :, 2 * i:2 * i + 2, :], y[:, 2 * i:2 * i + 2, :]).then_inc(s_out, 16)
                sp.wait_ge(s_out, (b + 1) * 16 * (T // 2))

        @block.gpsimd
        def _(pool):
            pool.memset(ident[:], 0.0).then_inc(s_const, 1)
            pool.memset(ident_b[:], 0.0).then_inc(s_const, 1)
            pool.memset(mask[:], 0.0).then_inc(s_const, 1)
            for i in range(3):
                last = pool.memset(stk[i][:].bitcast(F32), -1.0)
            last.then_inc(s_const, 1)
            pool.memset(va[:], 1.0).then_inc(s_const, 1)
            pool.wait_ge(s_const, 5)
            pool.affine_select(out=ident[:], in_=ident[:], compare_op=ALU.not_equal, fill=1.0, base=0,
                               pattern=[[-1, P]], channel_multiplier=1).then_inc(s_const, 1)
            pool.affine_select(out=ident_b[:], in_=ident_b[:], compare_op=ALU.not_equal, fill=1.0, base=0,
                               pattern=[[-1, P]], channel_multiplier=1).then_inc(s_const, 1)
            pool.affine_select(out=mask[:], in_=mask[:], compare_op=ALU.is_ge, fill=MASKED, base=0,
                               pattern=[[-1, P]], channel_multiplier=1).then_inc(s_const, 1)
            bo = flat[:, D:2 * D]
            for b in range(NB):
                if b == 0:
                    pool.wait_ge(s_w, 160)
                for i in range(4):
                    pool.wait_ge(s_x[i], 16 * (b + 1))
                for t in range(T):
                    pool.tensor_tensor(x_bo[:, t, :], x_in[:, t, :], bo, ALU.add).then_inc(s_xbo, 1)
                n = 0
                for g in range(G):
                    for s in diagonal:
                        q0 = steps[s][2]
                        k = n_step(g, s)
                        blk = pr[(k - 1) % 3][:, :, q0 % CHUNK:q0 % CHUNK + P]
                        pool.wait_ge(s_exp, HPG * (b * G * ST + k))
                        pool.affine_select(out=blk, in_=blk, compare_op=ALU.is_ge, fill=0.0, base=0,
                                           pattern=[[0, HPG], [1, P]], channel_multiplier=-1).then_inc(s_causal, 1)
                pool.wait_ge(s_out, (b + 1) * 16 * (T // 2))

        @block.scalar
        def _(act):
            act.wait_ge(s_w, 160)

            def empty(b, k, dst, func, **kw):
                act.wait_ge(s_ra, b * A + in_a[k] + 1)
                nc.scalar.activation(dst, bank_a(k), func, **kw).then_inc(s_ra_free, 1)

            for b in range(NB):
                for k in ring_a[0]:
                    _, c, kc = k
                    empty(b, k, xt[:, c, kc, :], ACT.Identity, scale=cols[:, 0, kc:kc + 1], bias=cols[:, 1, kc:kc + 1])
                for k in project:
                    _, m, c, w = k
                    act.wait_ge(s_rd, b * AD + in_d[k] + 1)
                    nc.scalar.activation(qk[:, m, w, 0, c * CHUNK:(c + 1) * CHUNK].bitcast(F32R), bank_d(k),
                                         ACT.Identity, bias=cols[:, 2 + w, m:m + 1]).then_inc(s_high, 1)
                for ev in plan:
                    if ev[0] == "score":
                        _, g, s, j = ev
                        k = n_step(g, s)
                        c, kt, q0, _ = steps[s]
                        w = (c + 1) * CHUNK - q0
                        n = HPG * (k - 1) + j
                        if j == 0 and k > 3:
                            act.wait_ge(s_value, b * G * ST + k - 3)
                        act.wait_ge(s_score, b * HPG * G * ST + n + 1)
                        nc.scalar.activation(pr[(k - 1) % 3][:, j, CHUNK - w:], ps[:, 4 + n % 2, CHUNK - w:],
                                             ACT.Exp, scale=DH ** -0.5).then_inc(s_exp, 1)
                    if ev[0] == "drain":
                        _, g, c = ev
                        n = g * C + c
                        act.wait_ge(s_value, b * G * ST + n_step(g, [i for i, s in enumerate(steps) if s[0] == c][-1]))
                        if n >= 2:
                            act.wait_ge(s_misc, b * MISC + n_misc[("turn", *divmod(n - 2, C))])
                        nc.scalar.activation(av_raw[:, n % 2, :], ps[:, 6, :], ACT.Copy).then_inc(s_drain, 1)
                for k in ring_a[1]:
                    if k[0] == "ot":
                        empty(b, k, o_t[:, k[2], k[1] * CHUNK:(k[1] + 1) * CHUNK], ACT.Copy)
                    if k[0] == "x1t":
                        empty(b, k, x1_t[:, k[2], k[1] * CHUNK:(k[1] + 1) * CHUNK], ACT.Copy)
                    if k[0] == "h":
                        empty(b, k, h_t[:, k[2], k[1] * CHUNK:(k[1] + 1) * CHUNK], ACT.Relu, bias=cols[:, 4, k[2]:k[2] + 1])
                    if k[0] == "avt":
                        if k[1] == 0:
                            for c in range(C):
                                act.wait_ge(s_lg, b * C + c + 1)
                                nc.scalar.activation(le[:, c], lg[:, c], ACT.Exp).then_inc(s_le, 1)
                        if k[1] >= 2:
                            act.wait_ge(s_rd, b * AD + in_d[("u", k[1] - 2)] + 1)
                        empty(b, k, avt[:, k[1] % 2, :], ACT.Copy)
                act.wait_ge(s_out, (b + 1) * 16 * (T // 2))

        @block.vector
        def _(dve):
            done = [0]

            def link(ins):
                done[0] += 1
                ins.then_inc(s_dve, 1)
                dve.wait_ge(s_dve, done[0])

            def make_rstd(c):
                v, i, yy, t = (nv[:, n, :] for n in range(4))
                link(nc.vector.tensor_scalar(v, mv[:, c * TPC:(c + 1) * TPC, 1], LN_EPS, None, ALU.add))
                link(nc.vector.tensor_scalar(i.bitcast(I32), v.bitcast(I32), 1, None, ALU.logical_shift_right))
                link(nc.vector.tensor_scalar(yy.bitcast(I32), i.bitcast(I32), -1.0, RSQRT_MAGIC, ALU.mult, ALU.add))
                for step in range(3):
                    link(nc.vector.tensor_tensor(t, yy, yy, ALU.mult))
                    link(nc.vector.scalar_tensor_tensor(i, t, -0.5, v, ALU.mult, ALU.mult))
                    dst = rstd[:, c * TPC:(c + 1) * TPC] if step == 2 else yy
                    link(nc.vector.scalar_tensor_tensor(dst, i, 1.5, yy, ALU.add, ALU.mult))

            def stats(src, t):
                link(nc.vector.bn_stats(st6[:, t, :], src))
                return nc.vector.bn_aggr(mv[:, t, :], st6[:, t, :])

            def normalize(dst, src, t):
                return nc.vector.tensor_scalar(dst, src, mv[:, t, 0:1], rstd[:, t:t + 1], ALU.subtract, ALU.mult)

            dve.wait_ge(s_w, 160)
            for b in range(NB):
                for c in range(C):
                    for t in range(c * TPC, (c + 1) * TPC):
                        if t % 2 == 0:
                            dve.wait_ge(s_x[t // 2], 16 * (b + 1))
                        link(stats(x_in[:, t, :], t))
                    make_rstd(c)
                    for t in range(c * TPC, (c + 1) * TPC):
                        ins = normalize(xh[:, t, :], x_in[:, t, :], t)
                    ins.then_inc(s_xh, 1)
                for i, k in enumerate(project):
                    _, m, c, w = k
                    dve.wait_ge(s_high, b * len(project) + i + 1)
                    part = qk[:, m, w, :, c * CHUNK:(c + 1) * CHUNK]
                    ins = nc.vector.scalar_tensor_tensor(part[:, 1].bitcast(F32R), bank_d(k), cols[:, 2 + w, m:m + 1],
                                                         part[:, 0], ALU.add, ALU.subtract)
                    ins.then_inc(s_rd_free, 1)
                for t in range(0, T, 2):
                    k = ("v", t)
                    dve.wait_ge(s_rd, b * AD + in_d[k] + 1)
                    if t == 0 and b == 0:
                        dve.wait_ge(s_const, 8)
                    for i in range(2):
                        ins = nc.vector.tensor_tensor(
                            va[:, t + i, :, 0:DH],
                            bank_d(k)[:, i * D:(i + 1) * D].rearrange("p (h d) -> p h d", h=HEADS),
                            flat[:, 0:D].rearrange("p (h d) -> p h d", h=HEADS), ALU.add)
                    ins.then_inc(s_rd_free, 1)
                for ev in plan:
                    if ev[0] == "max":
                        _, g, u = ev
                        t, heads, w = units[u]
                        dve.wait_ge(s_max, b * G * U + n_unit(g, u))
                        bank = max_bank(g, u)
                        h0, n = heads[0], len(heads)
                        dst = mx[:, g % 2, :].rearrange("p (h a t) -> p h a t", h=2, a=PAIRS)
                        if w <= 256:
                            src = bank[:, :, 0:PAIRS * w].rearrange("p h (a k) -> p h a k", k=w)
                            nc.vector.tensor_reduce(dst[:, :, :, t], src, AX.X, ALU.max).then_inc(s_maxed, 1)
                        elif w <= CHUNK:
                            nc.vector.tensor_reduce(dst[:, :, h0 // 2, t], bank[:, :, 0:w], AX.X, ALU.max).then_inc(s_maxed, 1)
                        else:
                            src = bank.rearrange("p b c -> p (b c)")[:, 0:w]
                            nc.vector.tensor_reduce(dst[:, h0 % 2, h0 // 2, t:t + 1], src, AX.X, ALU.max).then_inc(s_maxed, 1)
                        if u == U - 1:
                            dve.wait_ge(s_maxed, b * G * U + n_unit(g, u))
                            if g or b:
                                dve.wait_ge(s_misc, b * MISC + (n_misc[("rows", g - 1)] if g else 0))
                            link(nc.vector.tensor_copy(mhl[:, 0, :], mx[:, g % 2, :]))
                            nc.vector.tensor_tensor(mhl[:, 1, :], mx[:, g % 2, :], mhl[:, 0, :].bitcast(F32),
                                                    ALU.subtract).then_inc(s_mhl, 1)
                    if ev[0] == "rows":
                        g = ev[1]
                        dve.wait_ge(s_misc, b * MISC + n_misc[ev])
                        if g or b:
                            dve.wait_ge(s_mrow, 64 * (b * G + g))
                        nc.vector.tensor_copy(mrow[:, :], ps[0:2 * HPG * T, 7, 0:P]).then_inc(s_misc_free, 1)
                    if ev[0] == "turn":
                        _, g, c = ev
                        dve.wait_ge(s_misc, b * MISC + n_misc[ev])
                        o4 = ps[:, 7, :].rearrange("p (t h v) -> p t h v", t=TPC, h=HPG)
                        link(nc.vector.reciprocal(rs[:], o4[:, :, :, DH]))
                        nc.vector.tensor_tensor(
                            o_sb[:, c * TPC:(c + 1) * TPC, g * HPG * DH:(g + 1) * HPG * DH].rearrange(
                                "p t (h d) -> p t h d", h=HPG),
                            o4[:, :, :, 0:DH], rs[:].unsqueeze(3).to_broadcast([P, TPC, HPG, DH]),
                            ALU.mult).then_inc(s_misc_free, 1)
                for c in range(C):
                    for t in range(c * TPC, (c + 1) * TPC, 2):
                        k = ("r1", t)
                        dve.wait_ge(s_rd, b * AD + in_d[k] + 1)
                        dve.wait_ge(s_xbo, b * T + t + 2)
                        nc.vector.tensor_tensor(r1[:, t:t + 2, :], bank_d(k).rearrange("p (t d) -> p t d", t=2),
                                                x_bo[:, t:t + 2, :], ALU.add).then_inc(s_rd_free, 1)
                        dve.wait_ge(s_rd_free, b * AD + in_d[k] + 1)
                        for i in range(2):
                            link(stats(r1[:, t + i, :], t + i))
                    make_rstd(c)
                    for t in range(c * TPC, (c + 1) * TPC):
                        ins = normalize(x1[:, t, :], r1[:, t, :], t)
                    ins.then_inc(s_x1, 1)
                for c in range(C):
                    k = ("lg", c)
                    dve.wait_ge(s_rd, b * AD + in_d[k] + 1)
                    b2 = flat[:, 2 * D:].unsqueeze(1).to_broadcast([P, TPC, E])
                    nc.vector.tensor_tensor(lg[:, c], bank_d(k)[:, 0:TPC * E].rearrange("p (t e) -> p t e", t=TPC), b2,
                                            ALU.add).then_inc(s_rd_free, 1)
                    dve.wait_ge(s_rd_free, b * AD + in_d[k] + 1)
                    link(nc.vector.tensor_reduce(sm[:, c], lg[:, c], AX.X, ALU.max))
                    nc.vector.tensor_tensor(lg[:, c], lg[:, c], sm[:, c].unsqueeze(2).to_broadcast([P, TPC, E]),
                                            ALU.subtract).then_inc(s_lg, 1)
                for c in range(C):
                    dve.wait_ge(s_le, b * C + c + 1)
                    link(nc.vector.tensor_reduce(sm[:, c], le[:, c], AX.X, ALU.add))
                    link(nc.vector.reciprocal(sm[:, c], sm[:, c]))
                    link(nc.vector.tensor_tensor(alpha[:, c], le[:, c], sm[:, c].unsqueeze(2).to_broadcast([P, TPC, E]),
                                                 ALU.mult))
                for k in ffn:
                    t = k[1]
                    if k[0] == "vx":
                        dve.wait_ge(s_rd, b * AD + in_d[k] + 1)
                        if t >= 2:
                            dve.wait_ge(s_ra, b * A + in_a[("avt", t - 2)] + 1)
                        nc.vector.tensor_tensor(
                            avx[:, t % 2, :].rearrange("p (e r) -> p e r", e=E),
                            bank_d(k).rearrange("p (e r) -> p e r", e=E),
                            alpha[:, t // TPC, t % TPC, :].unsqueeze(2).to_broadcast([P, E, ER // E]),
                            ALU.mult).then_inc(s_rd_free, 1)
                    if k[0] == "u":
                        dve.wait_ge(s_rd, b * AD + in_d[k] + 1)
                        nc.vector.tensor_tensor(r2[:, t, :], bank_d(k)[:, 0:D], x1[:, t, :], ALU.add).then_inc(s_rd_free, 1)
                        dve.wait_ge(s_rd_free, b * AD + in_d[k] + 1)
                        link(stats(r2[:, t, :], t))
                        if t % TPC == TPC - 1:
                            make_rstd(t // TPC)
                            for i in range(t + 1 - TPC, t + 1):
                                normalize(y[:, i, :], r2[:, i, :], i).then_inc(s_y, 1)
                dve.wait_ge(s_out, (b + 1) * 16 * (T // 2))

        @block.tensor
        def _(pe):
            pe.wait_ge(s_w, 160)
            pe.wait_ge(s_const, 8)

            def take_a(b, k):
                if in_a[k] >= 4:
                    pe.wait_ge(s_ra_free, b * A + in_a[k] - 3)
                return bank_a(k)

            def take_d(b, k):
                if in_d[k] >= 4:
                    pe.wait_ge(s_rd_free, b * AD + in_d[k] - 3)
                return bank_d(k)

            def turn(bank, src, c, kc):
                for i in range(TPC):
                    last = nc.tensor.transpose(bank[:, i * P:(i + 1) * P], src[:, c * TPC + i, kc * P:(kc + 1) * P], ident[:])
                return last

            for b in range(NB):
                def project_chunk(k):
                    _, m, c, w = k
                    bank = take_d(b, k)
                    if w == 0:
                        pe.wait_ge(s_ra_free, b * A + in_a[("xt", c, KC - 1)] + 1)
                    for kc in range(KC):
                        last = nc.tensor.matmul(bank, w_qk[:, kc, w, m * P:(m + 1) * P], xt[:, c, kc, :],
                                                start=(kc == 0), stop=(kc == KC - 1))
                    last.then_inc(s_rd, 1)

                for c in range(C):
                    pe.wait_ge(s_xh, b * C + c + 1)
                    for kc in range(KC):
                        turn(take_a(b, ("xt", c, kc)), xh, c, kc).then_inc(s_ra, 1)
                    if c == 0:
                        project_chunk(project[0])
                        project_chunk(project[1])
                for k in project[2:]:
                    project_chunk(k)
                for t in range(0, T, 2):
                    bank = take_d(b, ("v", t))
                    for i in range(2):
                        for kc in range(KC):
                            last = nc.tensor.matmul(bank[:, i * D:(i + 1) * D],
                                                    xt[:, (t + i) // TPC, kc, (t + i) % TPC * P:((t + i) % TPC + 1) * P],
                                                    w_v[:, kc, :], start=(kc == 0), stop=(kc == KC - 1))
                    last.then_inc(s_rd, 1)

                pe.wait_ge(s_ra_free, b * A + len(ring_a[0]))
                pe.wait_ge(s_rd_free, b * AD + len(ring_d[0]))

                for ev in plan:
                    if ev[0] == "max":
                        _, g, u = ev
                        t, heads, w = units[u]
                        if u == 0:
                            pe.wait_ge(s_stack[g], (b + 1) * 16 * HPG * 6)
                        if n_unit(g, u) > 2:
                            pe.wait_ge(s_maxed, b * G * U + n_unit(g, u) - 2)
                        bank = max_bank(g, u).rearrange("p b c -> p (b c)")
                        for j in heads:
                            lo = 64 * (j % 2)
                            place = 0 if w > CHUNK else CHUNK * (j % 2) + (w * (j // 2) if w <= 256 else 0)
                            for k0 in range(0, w, CHUNK):
                                kw = min(CHUNK, w - k0)
                                at = place + k0
                                rows_ = slice(lo, lo + 3 * DH)
                                nc.tensor.matmul(bank[:, at:at + kw],
                                                 stq[g % 3][rows_, j // 2, t * P:(t + 1) * P],
                                                 stk[g % 3][rows_, j // 2, k0:k0 + kw],
                                                 start=True, stop=(k0 + kw < w))
                                if k0 + kw == w:
                                    last = nc.tensor.matmul(bank[:, at + kw - P:at + kw], ident_b[:], mask[:],
                                                            start=False, stop=True)
                        last.then_inc(s_max, 1)
                    if ev[0] == "rows":
                        g = ev[1]
                        pe.wait_ge(s_mhl, b * G + g + 1)
                        if n_misc[ev] > 1:
                            pe.wait_ge(s_misc_free, b * MISC + n_misc[ev] - 1)
                        nc.tensor.transpose(ps[0:2 * HPG * T, 7, 0:P], mhl[:].rearrange("p a n -> p (a n)").bitcast(F32),
                                            ident[:]).then_inc(s_misc, 1)
                    if ev[0] == "score":
                        _, g, s, j = ev
                        c, kt, q0, _ = steps[s]
                        n = HPG * (n_step(g, s) - 1) + j
                        if s == 0 and j == 0:
                            pe.wait_ge(s_mrow, 64 * (b * G + g + 1))
                        if n >= 2:
                            pe.wait_ge(s_exp, b * HPG * G * ST + n - 1)
                        w = (c + 1) * CHUNK - q0
                        rows_ = slice(64 * (j % 2), 64 * (j % 2) + KROWS)
                        nc.tensor.matmul(ps[:, 4 + n % 2, CHUNK - w:], stk[g % 3][rows_, j // 2, kt * P:(kt + 1) * P],
                                         stq[g % 3][rows_, j // 2, q0:q0 + w], start=True, stop=True).then_inc(s_score, 1)
                    if ev[0] == "value":
                        _, g, s = ev
                        c, kt, q0, ends = steps[s]
                        k = n_step(g, s)
                        w = (c + 1) * CHUNK - q0
                        if s in diagonal:
                            pe.wait_ge(s_causal, b * G * len(diagonal) + g * len(diagonal) + diagonal.index(s) + 1)
                        else:
                            pe.wait_ge(s_exp, HPG * (b * G * ST + k))
                        if kt == 0 and g * C + c > 0:
                            pe.wait_ge(s_drain, b * G * C + g * C + c)
                        for j in range(HPG):
                            last = nc.tensor.matmul(ps[j * VW:(j + 1) * VW, 6, CHUNK - w:], va[:, kt, g * HPG + j, :],
                                                    pr[(k - 1) % 3][:, j, CHUNK - w:], start=(kt == 0), stop=ends)
                        last.then_inc(s_value, 1)
                    if ev[0] == "turn":
                        _, g, c = ev
                        pe.wait_ge(s_drain, b * G * C + g * C + c + 1)
                        if n_misc[ev] > 1:
                            pe.wait_ge(s_misc_free, b * MISC + n_misc[ev] - 1)
                        for i in range(TPC):
                            last = nc.tensor.transpose(ps[:, 7, i * P:(i + 1) * P],
                                                       av_raw[:, (g * C + c) % 2, i * P:(i + 1) * P], ident[:])
                        last.then_inc(s_misc, 1)

                pe.wait_ge(s_maxed, (b + 1) * G * U)
                pe.wait_ge(s_misc_free, (b + 1) * MISC)

                for c in range(C):
                    for kc in range(KC):
                        turn(take_a(b, ("ot", c, kc)), o_sb, c, kc).then_inc(s_ra, 1)
                for t in range(0, T, 2):
                    bank = take_d(b, ("r1", t))
                    pe.wait_ge(s_ra_free, b * A + in_a[("ot", t // TPC, KC - 1)] + 1)
                    for i in range(2):
                        for kc in range(KC):
                            last = nc.tensor.matmul(bank[:, i * D:(i + 1) * D], o_t[:, kc, (t + i) * P:(t + i + 1) * P],
                                                    w_o[:, kc, :], start=(kc == 0), stop=(kc == KC - 1))
                    last.then_inc(s_rd, 1)
                for c in range(C):
                    pe.wait_ge(s_x1, b * C + c + 1)
                    for kc in range(KC):
                        turn(take_a(b, ("x1t", c, kc)), x1, c, kc).then_inc(s_ra, 1)
                    pe.wait_ge(s_ra_free, b * A + in_a[("x1t", c, KC - 1)] + 1)
                    for m in range(KC):
                        bank = take_a(b, ("h", c, m))
                        for kc in range(KC):
                            last = nc.tensor.matmul(bank, w_1[:, kc, m * P:(m + 1) * P],
                                                    x1_t[:, kc, c * CHUNK:(c + 1) * CHUNK],
                                                    start=(kc == 0), stop=(kc == KC - 1))
                        last.then_inc(s_ra, 1)
                for c in range(C):
                    bank = take_d(b, ("lg", c))
                    pe.wait_ge(s_ra_free, b * A + in_a[("h", c, KC - 1)] + 1)
                    for i in range(TPC):
                        t = c * TPC + i
                        for kc in range(KC):
                            last = nc.tensor.matmul(bank[:, i * E:(i + 1) * E], h_t[:, kc, t * P:(t + 1) * P],
                                                    w_2[:, kc, :], start=(kc == 0), stop=(kc == KC - 1))
                    last.then_inc(s_rd, 1)
                for k in ffn:
                    t = k[1]
                    if k[0] == "vx":
                        bank = take_d(b, k)
                        for kc in range(KC):
                            last = nc.tensor.matmul(bank, x1_t[:, kc, t * P:(t + 1) * P], v_t[:, kc, :],
                                                    start=(kc == 0), stop=(kc == KC - 1))
                        last.then_inc(s_rd, 1)
                    if k[0] == "avt":
                        bank = take_a(b, k)
                        pe.wait_ge(s_rd_free, b * AD + in_d[("vx", t)] + 1)
                        for r in range(RC):
                            last = nc.tensor.transpose(bank[:, r * P:(r + 1) * P], avx[:, t % 2, r * P:(r + 1) * P], ident[:])
                        last.then_inc(s_ra, 1)
                    if k[0] == "u":
                        bank = take_d(b, k)
                        pe.wait_ge(s_ra_free, b * A + in_a[("avt", t)] + 1)
                        for r in range(RC):
                            last = nc.tensor.matmul(bank[:, 0:D], avt[:, t % 2, r * P:(r + 1) * P], u_t[:, r, :],
                                                    start=(r == 0), stop=(r == RC - 1))
                        last.then_inc(s_rd, 1)
                pe.wait_ge(s_out, (b + 1) * 16 * (T // 2))


def kernel(**inputs):
    import numpy as np
    import concourse.bacc as bacc
    from concourse.bass_utils import run_bass_kernel_spmd

    a = {k: np.asarray(v) for k, v in inputs.items()}
    x = a["L0_attn_X"]
    D = x.shape[-1]
    n = D // P

    def by_partition(v):
        return v.reshape(n, P).T

    vecs = np.concatenate([by_partition(a[k]) for k in
                           ("L0_attn_ln_g", "L0_attn_ln_b", "L0_attn_bq", "L0_attn_bk", "L0_ffn_b1")], axis=1)
    rows = np.concatenate([a["L0_attn_bv"], a["L0_attn_bo"], a["L0_ffn_b2"]])
    ins = {
        "x": x, "vecs": vecs, "rows": rows,
        "wq": a["L0_attn_Wq"], "wk": a["L0_attn_Wk"], "wv": a["L0_attn_Wv"], "wo": a["L0_attn_Wo"],
        "w1": a["L0_ffn_W1"], "w2": a["L0_ffn_W2"],
        "vt": a["L0_ffn_V"].transpose(2, 0, 1).reshape(D, -1),
        "ut": a["L0_ffn_U"].transpose(0, 2, 1).reshape(-1, D),
    }
    nc = bacc.Bacc("TRN2", target_bir_lowering=False, num_devices=1)
    arrays, args = {}, []
    for name, v in ins.items():
        v = np.ascontiguousarray(v)
        arrays[f"in_{name}"] = v
        args.append(nc.dram_tensor(f"in_{name}", v.shape, mybir.dt.from_np(v.dtype), kind="ExternalInput").ap())
    out = nc.dram_tensor("out_y", x.shape, mybir.dt.from_np(x.dtype), kind="ExternalOutput").ap()
    block_kernel(nc, *args, out)
    r = run_bass_kernel_spmd(nc, [arrays], core_ids=[0])
    return r.results[0]["out_y"]
```

```python
from contextlib import ExitStack

import concourse.bass as bass
from concourse import mybir

ALU = mybir.AluOpType
ACT = mybir.ActivationFunctionType
AX = mybir.AxisListType
F32 = mybir.dt.float32
F32R = mybir.dt.float32r
BF16 = mybir.dt.bfloat16
I32 = mybir.dt.int32

P = 128
HEADS = 16
DH = 16
HPG = 4
VW = 32
CHUNK = 512
TPC = CHUNK // P
LN_EPS = 1e-5
MASKED = -1e30
RSQRT_MAGIC = float(0x5F3759DF)
RING = 3
STACKS = 3
PROBS = 3
PARTS = 3
HALF = PARTS * DH


def max_units(tiles):
    units = []
    for t in range(tiles):
        for k0 in range(0, (t + 1) * P, CHUNK):
            w = min(CHUNK, (t + 1) * P - k0)
            n = 4 if w == P else 2 if w == 2 * P else 1
            units += [(t, k0, w, tuple(range(j, j + n)), k0 + w == (t + 1) * P) for j in range(0, HPG, n)]
    return units


def score_steps(tiles):
    return [(c, kt, max(kt * P, c * CHUNK), kt == TPC * (c + 1) - 1)
            for c in range(tiles // TPC) for kt in range(TPC * (c + 1))]


def attention_order(b, groups, tiles, beside):
    units, steps = max_units(tiles), score_steps(tiles)
    U, ST = len(units), len(steps)
    per_chunk = [sum(u[0] // TPC == c for u in units) for c in range(tiles // TPC)]
    starts = [s for s in range(ST) if s == 0 or steps[s][0] != steps[s - 1][0]]
    order, issued, due = [], 0, []

    def issue_max(upto):
        nonlocal issued
        while issued < min(upto, groups * U):
            g, u = divmod(issued, U)
            order.append(("max", b, g, u))
            issued += 1
            c = units[u][0] // TPC
            if u == U - 1 or units[u + 1][0] // TPC != c:
                order.append(("split", b, g, c))
                due.append((issued + 3, g, c))
            while due and issued >= due[0][0]:
                order.append(("rows", b, *due.pop(0)[1:]))

    def target(k):
        first, second = per_chunk[0] + 6, U + 8
        if k < starts[1]:
            return first + (second - first) * k / starts[1]
        return second + (groups * U - second) * (k - starts[1]) / ((groups - 1) * ST - starts[1])

    issue_max(per_chunk[0] + 6)
    for k in range(groups * ST + 1):
        g, s = divmod(k, ST)
        for j in range(HPG):
            if k < groups * ST:
                if j == 0 and s in starts:
                    c = steps[s][0]
                    issue_max(g * U + sum(per_chunk[:c + 1]))
                    while due and (due[0][1], due[0][2]) <= (g, c):
                        order.append(("rows", b, *due.pop(0)[1:]))
                order.append(("score", b, g, s, j))
            issue_max(int(target(k + (j + 1) / HPG)))
            if k >= 2 and steps[(k - 2) % ST][3]:
                pg, pc = (k - 2) // ST, steps[(k - 2) % ST][0]
                if j == 1:
                    order.append(("drain", b, pg, pc))
                if j == 3:
                    order.append(("turn", b, pg, pc))
        if k:
            order.append(("value", b, *divmod(k - 1, ST)))
        order += beside.get(k, [])
    return order + [("drain", b, groups - 1, steps[-1][0]), ("turn", b, groups - 1, steps[-1][0])]


def program_order(batches, groups, tiles, parts):
    C = tiles // TPC
    ks, pairs = range(parts), range(0, tiles, 2)

    def chunk_tiles(c):
        return range(c * TPC, (c + 1) * TPC)

    def begin(b):
        o = []
        for c in range(C):
            o += [("xt", b, c, k) for k in ks]
            o += [("qk", b, m, c, w) for m in ks for w in range(2)]
            o.append(("stack", b, 0, c))
        return o + [("v", b, t) for t in pairs] + [("stack", b, g, c) for g in (1, 2) for c in range(C)]

    order = [("load", 0)] + [("ln1", 0, c) for c in range(C)]
    ST = len(score_steps(tiles))
    for b in range(batches):
        order += begin(b)
        last = (groups - 1) * ST
        beside = {
            last + 6: [("ot", b, 0, k) for k in ks] + [("r1", b, t) for t in pairs if t in chunk_tiles(0)] + [("ln2", b, 0)],
            last + 9: [("x1t", b, 0, k) for k in ks],
            last + 10: [("h", b, 0, k) for k in ks],
            last + 11: [("lg", b, 0)],
            last + 12: [("weigh", b, 0)],
        }
        for g in range(STACKS, groups):
            beside[(g - STACKS + 1) * ST] = [("stack", b, g, c) for c in range(C)]
        order += attention_order(b, groups, tiles, beside)
        order += [("ot", b, 1, k) for k in ks] + [("alpha", b, 0)]
        order += [("r1", b, t) for t in pairs if t in chunk_tiles(1)] + [("ln2", b, 1)]
        order += [("vx", b, 0), ("vx", b, 1), ("avt", b, 0), ("avt", b, 1)]
        order += [("x1t", b, 1, k) for k in ks] + [("h", b, 1, k) for k in ks] + [("lg", b, 1), ("weigh", b, 1)]
        if b + 1 < batches:
            order.append(("load", b + 1))
        order += [("vx", b, 2), ("u", b, 0), ("avt", b, 2), ("vx", b, 3), ("u", b, 1), ("alpha", b, 1)]
        for t in range(4, tiles + 2):
            order += [("vx", b, t)] * (t < tiles) + [("avt", b, t - 1)] * (t <= tiles) + [("u", b, t - 2)]
            if t == 6:
                order.append(("ln3", b, 0))
                order += [("ln1", b + 1, 0)] * (b + 1 < batches)
            if t == tiles - 1:
                order += [("ln1", b + 1, 1)] * (b + 1 < batches)
        order.append(("ln3", b, 1))
    return order


def block_kernel(nc, x, vecs, rows, wq, wk, wv, wo, w1, w2, vt, ut, out):
    NB, S, D = x.shape
    T = S // P
    C = S // CHUNK
    KC = D // P
    E = w2.shape[1]
    ER = vt.shape[1]
    RC = ER // P
    G = HEADS // HPG
    PAIRS = HPG // 2
    units, steps = max_units(T), score_steps(T)
    U, ST = len(units), len(steps)
    order = program_order(NB, G, T, KC)

    x_v = x.rearrange("b (t p) d -> b p t d", p=P)
    out_v = out.rearrange("b (t p) d -> b p t d", p=P)

    with ExitStack() as ctx:
        def sb(name, shape, dt=F32):
            return ctx.enter_context(nc.sbuf_tensor(name, shape, dt))

        def sem(name):
            return ctx.enter_context(nc.semaphore(name))

        w_qk = sb("w_qk", [P, KC, 2, D])
        w_v = sb("w_v", [P, KC, D])
        w_o = sb("w_o", [P, KC, D])
        w_1 = sb("w_1", [P, KC, D])
        w_2 = sb("w_2", [P, KC, E])
        v_t = sb("v_t", [P, KC, ER])
        u_t = sb("u_t", [P, RC, D])
        cols = sb("cols", [P, 5, KC])
        flat = sb("flat", [P, 2 * D + E])
        ident = sb("ident", [P, P])
        ident_b = sb("ident_b", [P, P], BF16)
        mask = sb("mask", [P, P], BF16)

        x_in = sb("x_in", [P, T, D])
        x1 = sb("x1", [P, T, D])
        qk = sb("qk", [P, 2, PARTS, C, KC, CHUNK])
        va = sb("va", [P, T, HEADS, VW])
        stq = [sb(f"stq{i}", [P, C, HPG, CHUNK], F32R) for i in range(STACKS)]
        stk = [sb(f"stk{i}", [P, C, PAIRS, CHUNK], F32R) for i in range(STACKS)]
        pr = [sb(f"pr{i}", [P, HPG, CHUNK]) for i in range(PROBS)]
        mx = sb("mx", [P, 2, 2, HPG, TPC])
        mhl = sb("mhl", [P, 2, 2, HPG, TPC], F32R)
        mrow = sb("mrow", [2 * HPG * TPC, 2, P], F32R)
        av_raw = sb("av_raw", [P, 2, CHUNK])
        rs = sb("rs", [P, TPC, HPG])
        st6 = sb("st6", [P, T, 6])
        mv = sb("mv", [P, T, 2])
        nv = sb("nv", [P, 4, TPC])
        rstd = sb("rstd", [P, T])
        lg = sb("lg", [P, C, TPC, E])
        le = sb("le", [P, C, TPC, E])
        sm = sb("sm", [P, C, TPC])
        alpha = sb("alpha", [P, C, TPC, E])

        qk_flat = qk[:].rearrange("p w r c m s -> p (w r c m s)")
        o_t, x1_t, h_t = (qk_flat[:, i * KC * S:(i + 1) * KC * S].rearrange("p (k s) -> p k s", k=KC) for i in range(3))
        xh, y = (pr[i][:].rearrange("p h (t d) -> p (h t) d", d=D) for i in range(2))
        o_sb = x1
        xt = pr[2][:].rearrange("p (c k) s -> p c k s", c=C)
        avx, avt = pr[2][:, 0:2, :], pr[2][:, 2:4, :]

        ps = ctx.enter_context(nc.psum_tensor("ps", [P, 8, CHUNK], F32))
        values_bank, turn_bank = ps[:, 6, :], ps[:, 7, :]

        s_cols = sem("s_cols")
        s_flat = sem("s_flat")
        s_w = {n: sem(f"s_w_{n}") for n in ("qk", "v", "o", "1", "2", "vt", "ut")}
        s_x = [sem(f"s_x{i}") for i in range(T // 2)]
        s_ident = sem("s_ident")
        s_mask = sem("s_mask")
        s_stack_init = sem("s_stack_init")
        s_minus = sem("s_minus")
        s_ones = sem("s_ones")
        s_bo = sem("s_bo")
        s_dve = sem("s_dve")
        s_xh = sem("s_xh")
        s_act_full = sem("s_act_full")
        s_act_free = sem("s_act_free")
        s_dve_full = sem("s_dve_full")
        s_dve_free = sem("s_dve_free")
        s_high = sem("s_high")
        s_copied = sem("s_copied")
        s_stack = [[sem(f"s_stack{i}_{c}") for c in range(C)] for i in range(STACKS)]
        s_split = sem("s_split")
        s_turned = sem("s_turned")
        s_turn_free = sem("s_turn_free")
        s_rows = [sem(f"s_rows{i}") for i in range(2)]
        s_causal = sem("s_causal")
        s_value = sem("s_value")
        s_drain = sem("s_drain")
        s_x1 = sem("s_x1_done")
        s_logits = sem("s_logits")
        s_weighed = sem("s_weighed")
        s_y = sem("s_y")
        s_out = sem("s_out")

        def count(*kinds):
            return {ev: n + 1 for n, ev in enumerate(e for e in order if e[0] in kinds)}

        n_act = count("xt", "score", "ot", "x1t", "h", "avt")
        n_dve = count("qk", "v", "max", "r1", "lg", "vx", "u")
        n_high = count("qk")
        n_ln1, n_ln2, n_weigh = count("ln1"), count("ln2"), count("weigh")
        n_logits = count("lg")
        n_split, n_rows = count("split"), count("rows")
        n_turn = count("rows", "turn")
        n_value, n_drain = count("value"), count("drain")
        on_diagonal = [s for s, (c, kt, q0, _) in enumerate(steps) if q0 == kt * P]
        n_causal = {ev: n + 1 for n, ev in enumerate(e for e in order if e[0] == "value" and e[3] in on_diagonal)}
        LOADS = 16 * 3

        def act_bank(ev):
            return ps[:, RING + (n_act[ev] - 1) % RING, :]

        def dve_bank(ev):
            return ps[:, (n_dve[ev] - 1) % RING, :]

        def probs(b, g, s):
            return pr[(n_value["value", b, g, s] - 1) % PROBS]

        def stack_of(b, g):
            return (b * G + g) % STACKS

        def last_step(c):
            return [s for s in range(ST) if steps[s][0] == c][-1]

        def span(c):
            return slice(c * CHUNK, (c + 1) * CHUNK)

        def tile(t):
            return slice(t * P, (t + 1) * P)

        block = ctx.enter_context(nc.Block())

        @block.sync
        def _(sp):
            def weight(dst, src, name):
                sp.dma_start(dst, src.rearrange("(k p) n -> p k n", p=P)).then_inc(s_w[name], 16)

            for ev in order:
                kind, b = ev[:2]
                if kind == "load":
                    for i in range(T // 2):
                        if b and i == 0:
                            sp.wait_ge(s_x1, n_ln2["ln2", b - 1, C - 1])
                        sp.dma_start(x_in[:, 2 * i:2 * i + 2, :], x_v[b, :, 2 * i:2 * i + 2, :]).then_inc(s_x[i], 16)
                        if b == 0 and i == 1:
                            sp.dma_start(cols[:], vecs.rearrange("p (v k) -> p v k", v=5)).then_inc(s_cols, 16)
                            weight(w_qk[:, :, 0, :], wq, "qk")
                            weight(w_qk[:, :, 1, :], wk, "qk")
                    if b == 0:
                        sp.dma_start(flat[:], rows.partition_broadcast(P)).then_inc(s_flat, 16)
                        weight(w_v[:], wv, "v")
                if kind == "stack":
                    _, _, g, c = ev
                    sp.wait_ge(s_dve_free, n_dve["qk", b, KC - 1, c, 1])
                    sp.wait_ge(s_copied, n_high["qk", b, KC - 1, c, 1])
                    n = b * G + g
                    if n < STACKS:
                        sp.wait_ge(s_stack_init, n + 1)
                    else:
                        sp.wait_ge(s_value, n_value["value", *divmod(n - STACKS, G), ST - 1])
                    loaded = s_stack[stack_of(b, g)][c]
                    sp.dma_start(stk[stack_of(b, g)][0:2 * HALF, c].bitcast(F32),
                                 qk[g * 2 * DH:(g + 1) * 2 * DH, 1, :, c]).then_inc(loaded, 16)
                    for i in range(2):
                        at = (2 * g + i) * DH
                        sp.dma_start(stq[stack_of(b, g)][i * HALF:(i + 1) * HALF, c, 2 * i:2 * i + 2].bitcast(F32),
                                     qk[at:at + DH, 0, :, c]).then_inc(loaded, 16)
                    if n == 0 and c == C - 1:
                        weight(w_o[:], wo, "o")
                        weight(w_1[:], w1, "1")
                        weight(w_2[:], w2, "2")
                        weight(v_t[:], vt, "vt")
                        weight(u_t[:], ut, "ut")
                if kind == "rows":
                    _, _, g, c = ev
                    sp.wait_ge(s_turn_free, n_turn[ev])
                    sp.dma_start(stq[stack_of(b, g)][2 * HALF:2 * HALF + 2, c].bitcast(F32),
                                 mrow[:, c, :].bitcast(F32)).then_inc(s_rows[c], 16)
                if kind == "ln3":
                    c = ev[2]
                    for i in range(c * TPC // 2, (c + 1) * TPC // 2):
                        sp.wait_ge(s_y, b * T + 2 * i + 2)
                        sp.dma_start(out_v[b, :, 2 * i:2 * i + 2, :], y[:, 2 * i:2 * i + 2, :]).then_inc(s_out, 16)
            sp.wait_ge(s_out, NB * 16 * (T // 2))

        @block.gpsimd
        def _(pool):
            pool.memset(ident[:], 0.0).then_inc(s_ident, 1)
            pool.memset(stq[0][0:2 * HALF].bitcast(F32), 0.0).then_inc(s_stack_init, 1)
            pool.wait_ge(s_ident, 1)
            pool.affine_select(out=ident[:], in_=ident[:], compare_op=ALU.not_equal, fill=1.0, base=0,
                               pattern=[[-1, P]], channel_multiplier=1).then_inc(s_ident, 1)
            pool.memset(ident_b[:], 0.0).then_inc(s_mask, 1)
            pool.memset(mask[:], 0.0).then_inc(s_mask, 1)
            pool.wait_ge(s_mask, 2)
            pool.affine_select(out=ident_b[:], in_=ident_b[:], compare_op=ALU.not_equal, fill=1.0, base=0,
                               pattern=[[-1, P]], channel_multiplier=1).then_inc(s_mask, 1)
            pool.affine_select(out=mask[:], in_=mask[:], compare_op=ALU.is_ge, fill=MASKED, base=0,
                               pattern=[[-1, P]], channel_multiplier=1).then_inc(s_mask, 1)
            pool.memset(va[:, :, :, DH:], 1.0).then_inc(s_ones, 1)
            for i in range(1, STACKS):
                pool.memset(stq[i][0:2 * HALF].bitcast(F32), 0.0).then_inc(s_stack_init, 1)
            for ev in order:
                kind, b = ev[:2]
                if kind == "ln1":
                    c = ev[2]
                    pool.wait_ge(s_flat, 16)
                    pool.wait_ge(s_xh, n_ln1[ev])
                    for t in range(c * TPC, (c + 1) * TPC):
                        pool.tensor_tensor(x_in[:, t, :], x_in[:, t, :], flat[:, D:2 * D], ALU.add).then_inc(s_bo, 1)
                if kind == "qk":
                    _, _, m, c, w = ev
                    pool.wait_ge(s_high, n_high[ev])
                    pool.tensor_copy(qk[:, w, 1 + w, c, m], qk[:, w, 0, c, m]).then_inc(s_copied, 1)
                if kind == "value" and ev in n_causal:
                    _, _, g, s = ev
                    q0 = steps[s][2]
                    blk = probs(b, g, s)[:, :, q0 % CHUNK:q0 % CHUNK + P]
                    pool.wait_ge(s_act_free, n_act["score", b, g, s, HPG - 1])
                    pool.affine_select(out=blk, in_=blk, compare_op=ALU.is_ge, fill=0.0, base=0,
                                       pattern=[[0, HPG], [1, P]], channel_multiplier=-1).then_inc(s_causal, 1)

        @block.scalar
        def _(act):
            act.wait_ge(s_cols, 16)
            for ev in order:
                kind, b = ev[:2]
                if kind in ("xt", "ot", "x1t", "h"):
                    _, _, c, k = ev
                    act.wait_ge(s_act_full, n_act[ev])
                    if kind == "xt":
                        ins = nc.scalar.activation(xt[:, c, k, :], act_bank(ev), ACT.Identity,
                                                   scale=cols[:, 0, k:k + 1], bias=cols[:, 1, k:k + 1])
                    elif kind == "h":
                        ins = nc.scalar.activation(h_t[:, k, span(c)], act_bank(ev), ACT.Relu, bias=cols[:, 4, k:k + 1])
                    else:
                        ins = nc.scalar.activation((o_t if kind == "ot" else x1_t)[:, k, span(c)], act_bank(ev), ACT.Copy)
                    ins.then_inc(s_act_free, 1)
                if kind == "qk":
                    _, _, m, c, w = ev
                    act.wait_ge(s_dve_full, n_dve[ev])
                    nc.scalar.activation(qk[:, w, 0, c, m].bitcast(F32R), dve_bank(ev),
                                         ACT.Identity, bias=cols[:, 2 + w, m:m + 1]).then_inc(s_high, 1)
                if kind == "score":
                    _, _, g, s, j = ev
                    c, kt, q0, _ = steps[s]
                    n = n_value["value", b, g, s]
                    if j == 0 and n > PROBS:
                        act.wait_ge(s_value, n - PROBS)
                    if j == 0 and b and g == 0 and s == 0:
                        act.wait_ge(s_out, b * 16 * (T // 2))
                    act.wait_ge(s_act_full, n_act[ev])
                    nc.scalar.activation(probs(b, g, s)[:, j, q0 - c * CHUNK:], act_bank(ev)[:, q0 - c * CHUNK:],
                                         ACT.Exp, scale=DH ** -0.5).then_inc(s_act_free, 1)
                if kind == "drain":
                    _, _, g, c = ev
                    act.wait_ge(s_value, n_value["value", b, g, last_step(c)])
                    n = n_drain[ev]
                    if n > 2:
                        before = [e for e in order if e[0] == "drain"][n - 3]
                        act.wait_ge(s_turned, n_turn["turn", *before[1:]])
                    nc.scalar.activation(av_raw[:, n % 2, :], values_bank, ACT.Copy).then_inc(s_drain, 1)
                if kind == "weigh":
                    c = ev[2]
                    act.wait_ge(s_logits, n_logits["lg", b, c])
                    nc.scalar.activation(le[:, c], lg[:, c], ACT.Exp).then_inc(s_weighed, 1)
                if kind == "avt":
                    t = ev[2]
                    act.wait_ge(s_act_full, n_act[ev])
                    if t >= 2:
                        act.wait_ge(s_dve_full, n_dve["u", b, t - 2])
                    nc.scalar.activation(avt[:, t % 2, :], act_bank(ev), ACT.Copy).then_inc(s_act_free, 1)

        @block.vector
        def _(dve):
            done = [0]

            def link(ins):
                done[0] += 1
                ins.then_inc(s_dve, 1)
                dve.wait_ge(s_dve, done[0])

            def make_rstd(c):
                v, i, yy, t = (nv[:, n, :] for n in range(4))
                link(nc.vector.tensor_scalar(v, mv[:, c * TPC:(c + 1) * TPC, 1], LN_EPS, None, ALU.add))
                link(nc.vector.tensor_scalar(i.bitcast(I32), v.bitcast(I32), 1, None, ALU.logical_shift_right))
                link(nc.vector.tensor_scalar(yy.bitcast(I32), i.bitcast(I32), -1.0, RSQRT_MAGIC, ALU.mult, ALU.add))
                for step in range(3):
                    link(nc.vector.tensor_tensor(t, yy, yy, ALU.mult))
                    link(nc.vector.scalar_tensor_tensor(i, t, -0.5, v, ALU.mult, ALU.mult))
                    dst = rstd[:, c * TPC:(c + 1) * TPC] if step == 2 else yy
                    link(nc.vector.scalar_tensor_tensor(dst, i, 1.5, yy, ALU.add, ALU.mult))

            def layer_norm(c, dst, src, sem_, each=False):
                ts = range(c * TPC, (c + 1) * TPC)
                for t in ts:
                    ins = nc.vector.bn_stats(st6[:, t, :], src[:, t, :])
                link(ins)
                for t in ts:
                    ins = nc.vector.bn_aggr(mv[:, t, :], st6[:, t, :])
                link(ins)
                make_rstd(c)
                for t in ts:
                    ins = nc.vector.tensor_scalar(dst[:, t, :], src[:, t, :], mv[:, t, 0:1], rstd[:, t:t + 1],
                                                  ALU.subtract, ALU.mult)
                    if each or t == ts[-1]:
                        ins.then_inc(sem_, 1)

            for i in range(STACKS):
                nc.vector.memset(stk[i][2 * HALF:2 * HALF + 2].bitcast(F32), -1.0).then_inc(s_minus, 1)
            for ev in order:
                kind, b = ev[:2]
                if kind == "ln1":
                    c = ev[2]
                    for i in range(c * TPC // 2, (c + 1) * TPC // 2):
                        dve.wait_ge(s_x[i], 16 * (b + 1))
                    layer_norm(c, xh, x_in, s_xh)
                if kind == "qk":
                    _, _, m, c, w = ev
                    if n_high[ev] == 1:
                        dve.wait_ge(s_cols, 16)
                        dve.wait_ge(s_flat, 16)
                    dve.wait_ge(s_high, n_high[ev])
                    nc.vector.scalar_tensor_tensor(
                        qk[:, w, 2 - w, c, m].bitcast(F32R), dve_bank(ev), cols[:, 2 + w, m:m + 1],
                        qk[:, w, 0, c, m], ALU.add, ALU.subtract).then_inc(s_dve_free, 1)
                if kind == "v":
                    t = ev[2]
                    dve.wait_ge(s_dve_full, n_dve[ev])
                    nc.vector.tensor_tensor(
                        va[:, t:t + 2, :, 0:DH],
                        dve_bank(ev).rearrange("p (t h d) -> p t h d", t=2, h=HEADS),
                        flat[:, 0:D].rearrange("p (h d) -> p h d", h=HEADS).unsqueeze(1).to_broadcast([P, 2, HEADS, DH]),
                        ALU.add).then_inc(s_dve_free, 1)
                if kind == "max":
                    _, _, g, u = ev
                    t, k0, w, heads, _ = units[u]
                    dve.wait_ge(s_dve_full, n_dve[ev])
                    dst = mx[:, t // TPC, k0 // CHUNK, heads[0]:heads[-1] + 1, t % TPC]
                    src = dve_bank(ev)[:, 0:len(heads) * w].rearrange("p (h k) -> p h k", k=w)
                    nc.vector.tensor_reduce(dst, src, AX.X, ALU.max).then_inc(s_dve_free, 1)
                    last_max = n_dve[ev]
                if kind == "split":
                    _, _, g, c = ev
                    dve.wait_ge(s_dve_free, last_max)
                    whole = mx[:, c, 0]
                    if c:
                        link(nc.vector.tensor_tensor(whole, mx[:, c, 0], mx[:, c, 1], ALU.max))
                    if n_split[ev] > 2:
                        dve.wait_ge(s_turned, n_turn["rows", *divmod(b * G + g - 1, G), c])
                    link(nc.vector.tensor_copy(mhl[:, c, 0], whole))
                    nc.vector.tensor_tensor(mhl[:, c, 1], whole, mhl[:, c, 0].bitcast(F32),
                                            ALU.subtract).then_inc(s_split, 1)
                if kind == "rows":
                    _, _, g, c = ev
                    dve.wait_ge(s_turned, n_turn[ev])
                    if b * G + g:
                        dve.wait_ge(s_rows[c], 16 * (b * G + g))
                    nc.vector.tensor_copy(mrow[:, c, :], turn_bank[0:2 * HPG * TPC, 0:P]).then_inc(s_turn_free, 1)
                if kind == "turn":
                    _, _, g, c = ev
                    dve.wait_ge(s_turned, n_turn[ev])
                    o4 = turn_bank.rearrange("p (t h v) -> p t h v", t=TPC, h=HPG)
                    link(nc.vector.reciprocal(rs[:], o4[:, :, :, DH]))
                    nc.vector.tensor_tensor(
                        o_sb[:, c * TPC:(c + 1) * TPC, g * HPG * DH:(g + 1) * HPG * DH].rearrange(
                            "p t (h d) -> p t h d", h=HPG),
                        o4[:, :, :, 0:DH], rs[:].unsqueeze(3).to_broadcast([P, TPC, HPG, DH]),
                        ALU.mult).then_inc(s_turn_free, 1)
                if kind == "r1":
                    t = ev[2]
                    dve.wait_ge(s_dve_full, n_dve[ev])
                    dve.wait_ge(s_bo, b * T + t + 2)
                    nc.vector.tensor_tensor(x_in[:, t:t + 2, :], dve_bank(ev).rearrange("p (t d) -> p t d", t=2),
                                            x_in[:, t:t + 2, :], ALU.add).then_inc(s_dve_free, 1)
                    dve.wait_ge(s_dve_free, n_dve[ev])
                if kind == "ln2":
                    layer_norm(ev[2], x1, x_in, s_x1)
                if kind == "lg":
                    c = ev[2]
                    dve.wait_ge(s_dve_full, n_dve[ev])
                    b2 = flat[:, 2 * D:].unsqueeze(1).to_broadcast([P, TPC, E])
                    nc.vector.tensor_tensor(lg[:, c], dve_bank(ev)[:, 0:TPC * E].rearrange("p (t e) -> p t e", t=TPC), b2,
                                            ALU.add).then_inc(s_dve_free, 1)
                    dve.wait_ge(s_dve_free, n_dve[ev])
                    link(nc.vector.tensor_reduce(sm[:, c], lg[:, c], AX.X, ALU.max))
                    nc.vector.tensor_tensor(lg[:, c], lg[:, c], sm[:, c].unsqueeze(2).to_broadcast([P, TPC, E]),
                                            ALU.subtract).then_inc(s_logits, 1)
                if kind == "alpha":
                    c = ev[2]
                    dve.wait_ge(s_weighed, n_weigh["weigh", b, c])
                    link(nc.vector.tensor_reduce(sm[:, c], le[:, c], AX.X, ALU.add))
                    link(nc.vector.reciprocal(sm[:, c], sm[:, c]))
                    link(nc.vector.tensor_tensor(alpha[:, c], le[:, c], sm[:, c].unsqueeze(2).to_broadcast([P, TPC, E]),
                                                 ALU.mult))
                if kind == "vx":
                    t = ev[2]
                    dve.wait_ge(s_dve_full, n_dve[ev])
                    if t >= 2:
                        dve.wait_ge(s_act_full, n_act["avt", b, t - 2])
                    nc.vector.tensor_tensor(
                        avx[:, t % 2, :].rearrange("p (e r) -> p e r", e=E),
                        dve_bank(ev).rearrange("p (e r) -> p e r", e=E),
                        alpha[:, t // TPC, t % TPC, :].unsqueeze(2).to_broadcast([P, E, ER // E]),
                        ALU.mult).then_inc(s_dve_free, 1)
                if kind == "u":
                    t = ev[2]
                    dve.wait_ge(s_dve_full, n_dve[ev])
                    nc.vector.tensor_tensor(x1[:, t, :], dve_bank(ev)[:, 0:D], x1[:, t, :], ALU.add).then_inc(s_dve_free, 1)
                    last_sum = n_dve[ev]
                if kind == "ln3":
                    dve.wait_ge(s_dve_free, last_sum)
                    layer_norm(ev[2], y, x1, s_y, each=True)

        @block.tensor
        def _(pe):
            def take_act(ev):
                if n_act[ev] > RING:
                    pe.wait_ge(s_act_free, n_act[ev] - RING)
                return act_bank(ev)

            def take_dve(ev):
                if n_dve[ev] > RING:
                    pe.wait_ge(s_dve_free, n_dve[ev] - RING)
                return dve_bank(ev)

            def take_turn(ev):
                if n_turn[ev] > 1:
                    pe.wait_ge(s_turn_free, n_turn[ev] - 1)

            def weights(name, b, n=16):
                if b == 0:
                    pe.wait_ge(s_w[name], n)

            def turn(bank, src, c, k):
                for i in range(TPC):
                    last = nc.tensor.transpose(bank[:, tile(i)], src[:, c * TPC + i, tile(k)], ident[:])
                return last

            def product(out_, lhs, rhs, n):
                for k in range(n):
                    last = nc.tensor.matmul(out_, lhs(k), rhs(k), start=(k == 0), stop=(k == n - 1))
                return last

            pe.wait_ge(s_ident, 2)
            for ev in order:
                kind, b = ev[:2]
                if kind in ("xt", "ot", "x1t"):
                    _, _, c, k = ev
                    bank = take_act(ev)
                    if kind == "xt":
                        pe.wait_ge(s_xh, n_ln1["ln1", b, c])
                        src = xh
                    if kind == "ot":
                        pe.wait_ge(s_turn_free, n_turn["turn", b, G - 1, c])
                        src = o_sb
                    if kind == "x1t":
                        pe.wait_ge(s_x1, n_ln2["ln2", b, c])
                        src = x1
                    turn(bank, src, c, k).then_inc(s_act_full, 1)
                if kind == "qk":
                    _, _, m, c, w = ev
                    bank = take_dve(ev)
                    weights("qk", b, 32)
                    pe.wait_ge(s_act_free, n_act["xt", b, c, KC - 1])
                    product(bank, lambda k: w_qk[:, k, w, tile(m)], lambda k: xt[:, c, k, :], KC).then_inc(s_dve_full, 1)
                if kind == "v":
                    t = ev[2]
                    bank = take_dve(ev)
                    weights("v", b)
                    for i in range(2):
                        c, n = divmod(t + i, TPC)
                        last = product(bank[:, i * D:(i + 1) * D], lambda k: xt[:, c, k, tile(n)], lambda k: w_v[:, k, :], KC)
                    last.then_inc(s_dve_full, 1)
                if kind == "max":
                    _, _, g, u = ev
                    t, k0, w, heads, diagonal = units[u]
                    q, k = stq[stack_of(b, g)], stk[stack_of(b, g)]
                    if t % TPC == 0 and k0 == 0 and heads[0] == 0:
                        pe.wait_ge(s_stack[stack_of(b, g)][t // TPC], LOADS * ((b * G + g) // STACKS + 1))
                        if b == 0 and g == 0:
                            pe.wait_ge(s_mask, 4)
                    bank = take_dve(ev)
                    for i, j in enumerate(heads):
                        last = nc.tensor.matmul(bank[:, i * w:(i + 1) * w], q[0:2 * HALF, t // TPC, j, tile(t % TPC)],
                                                k[0:2 * HALF, k0 // CHUNK, j % 2, 0:w], start=True, stop=not diagonal)
                        if diagonal:
                            last = nc.tensor.matmul(bank[:, (i + 1) * w - P:(i + 1) * w], ident_b[:], mask[:],
                                                    start=False, stop=True)
                    last.then_inc(s_dve_full, 1)
                if kind == "rows":
                    _, _, g, c = ev
                    pe.wait_ge(s_split, n_split["split", b, g, c])
                    take_turn(ev)
                    nc.tensor.transpose(turn_bank[0:2 * HPG * TPC, 0:P],
                                        mhl[:, c].rearrange("p a h t -> p (a h t)").bitcast(F32),
                                        ident[:]).then_inc(s_turned, 1)
                if kind == "score":
                    _, _, g, s, j = ev
                    c, kt, q0, _ = steps[s]
                    if kt == 0 and j == 0:
                        if b == g == c == 0:
                            pe.wait_ge(s_minus, STACKS)
                        pe.wait_ge(s_rows[c], 16 * (b * G + g + 1))
                    bank = take_act(ev)
                    nc.tensor.matmul(bank[:, q0 - c * CHUNK:], stk[stack_of(b, g)][0:2 * HALF + 2, kt // TPC, j % 2, tile(kt % TPC)],
                                     stq[stack_of(b, g)][0:2 * HALF + 2, c, j, q0 - c * CHUNK:],
                                     start=True, stop=True).then_inc(s_act_full, 1)
                if kind == "value":
                    _, _, g, s = ev
                    c, kt, q0, ends = steps[s]
                    if ev in n_causal:
                        pe.wait_ge(s_causal, n_causal[ev])
                    else:
                        pe.wait_ge(s_act_free, n_act["score", b, g, s, HPG - 1])
                    if n_value[ev] == 1:
                        pe.wait_ge(s_ones, 1)
                    if kt == 0:
                        pe.wait_ge(s_dve_free, n_dve["v", b, T - 2])
                        if n_drain["drain", b, g, c] > 1:
                            pe.wait_ge(s_drain, n_drain["drain", b, g, c] - 1)
                    for j in range(HPG):
                        last = nc.tensor.matmul(values_bank[j * VW:(j + 1) * VW, q0 - c * CHUNK:],
                                                va[:, kt, g * HPG + j, :], probs(b, g, s)[:, j, q0 - c * CHUNK:],
                                                start=(kt == 0), stop=ends)
                    last.then_inc(s_value, 1)
                if kind == "turn":
                    _, _, g, c = ev
                    n = n_drain["drain", b, g, c]
                    pe.wait_ge(s_drain, n)
                    take_turn(ev)
                    for i in range(TPC):
                        last = nc.tensor.transpose(turn_bank[:, tile(i)], av_raw[:, n % 2, tile(i)], ident[:])
                    last.then_inc(s_turned, 1)
                if kind == "r1":
                    t = ev[2]
                    bank = take_dve(ev)
                    weights("o", b)
                    pe.wait_ge(s_act_free, n_act["ot", b, t // TPC, KC - 1])
                    for i in range(2):
                        last = product(bank[:, i * D:(i + 1) * D], lambda k: o_t[:, k, tile(t + i)], lambda k: w_o[:, k, :], KC)
                    last.then_inc(s_dve_full, 1)
                if kind == "h":
                    _, _, c, m = ev
                    bank = take_act(ev)
                    weights("1", b)
                    pe.wait_ge(s_act_free, n_act["x1t", b, c, KC - 1])
                    product(bank, lambda k: w_1[:, k, tile(m)], lambda k: x1_t[:, k, span(c)], KC).then_inc(s_act_full, 1)
                if kind == "lg":
                    c = ev[2]
                    bank = take_dve(ev)
                    weights("2", b)
                    pe.wait_ge(s_act_free, n_act["h", b, c, KC - 1])
                    for i in range(TPC):
                        last = product(bank[:, i * E:(i + 1) * E], lambda k: h_t[:, k, tile(c * TPC + i)],
                                       lambda k: w_2[:, k, :], KC)
                    last.then_inc(s_dve_full, 1)
                if kind == "vx":
                    t = ev[2]
                    bank = take_dve(ev)
                    weights("vt", b)
                    product(bank, lambda k: x1_t[:, k, tile(t)], lambda k: v_t[:, k, :], KC).then_inc(s_dve_full, 1)
                if kind == "avt":
                    t = ev[2]
                    bank = take_act(ev)
                    pe.wait_ge(s_dve_free, n_dve["vx", b, t])
                    for r in range(RC):
                        last = nc.tensor.transpose(bank[:, tile(r)], avx[:, t % 2, tile(r)], ident[:])
                    last.then_inc(s_act_full, 1)
                if kind == "u":
                    t = ev[2]
                    bank = take_dve(ev)
                    weights("ut", b)
                    pe.wait_ge(s_act_free, n_act["avt", b, t])
                    product(bank[:, 0:D], lambda k: avt[:, t % 2, tile(k)], lambda k: u_t[:, k, :], RC).then_inc(s_dve_full, 1)


def kernel(**inputs):
    import numpy as np
    import concourse.bacc as bacc
    from concourse.bass_utils import run_bass_kernel_spmd

    a = {k: np.asarray(v) for k, v in inputs.items()}
    x = a["L0_attn_X"]
    D = x.shape[-1]
    n = D // P

    def by_pairs(v):
        return v.reshape(-1, HEADS // HPG, 2, n, DH).transpose(0, 3, 1, 2, 4).reshape(v.shape)

    def by_partition(v):
        return v.reshape(n, P).T

    vecs = np.concatenate([by_partition(v) for v in (
        a["L0_attn_ln_g"], a["L0_attn_ln_b"], by_pairs(a["L0_attn_bq"]), by_pairs(a["L0_attn_bk"]), a["L0_ffn_b1"])], axis=1)
    rows = np.concatenate([a["L0_attn_bv"], a["L0_attn_bo"], a["L0_ffn_b2"]])
    ins = {
        "x": x, "vecs": vecs, "rows": rows,
        "wq": by_pairs(a["L0_attn_Wq"]), "wk": by_pairs(a["L0_attn_Wk"]), "wv": a["L0_attn_Wv"], "wo": a["L0_attn_Wo"],
        "w1": a["L0_ffn_W1"], "w2": a["L0_ffn_W2"],
        "vt": a["L0_ffn_V"].transpose(2, 0, 1).reshape(D, -1),
        "ut": a["L0_ffn_U"].transpose(0, 2, 1).reshape(-1, D),
    }
    nc = bacc.Bacc("TRN2", target_bir_lowering=False, num_devices=1)
    arrays, args = {}, []
    for name, v in ins.items():
        v = np.ascontiguousarray(v)
        arrays[f"in_{name}"] = v
        args.append(nc.dram_tensor(f"in_{name}", v.shape, mybir.dt.from_np(v.dtype), kind="ExternalInput").ap())
    out = nc.dram_tensor("out_y", x.shape, mybir.dt.from_np(x.dtype), kind="ExternalOutput").ap()
    block_kernel(nc, *args, out)
    r = run_bass_kernel_spmd(nc, [arrays], core_ids=[0])
    return r.results[0]["out_y"]
```

```python
from contextlib import ExitStack

import concourse.bass as bass
from concourse import mybir

ALU = mybir.AluOpType
ACT = mybir.ActivationFunctionType
AX = mybir.AxisListType
F32 = mybir.dt.float32
F32R = mybir.dt.float32r
BF16 = mybir.dt.bfloat16
I32 = mybir.dt.int32

P = 128
HEADS = 16
DH = 16
HPG = 4
VW = 32
CHUNK = 512
TPC = CHUNK // P
LN_EPS = 1e-5
MASKED = -1e30
RSQRT_MAGIC = float(0x5F3759DF)
DVE_RING, ACT_RING = 4, 3
STACKS = 3
PROBS = 3
ROWS = 2 * 3 * DH


def max_units(tiles):
    units = []
    for t in range(tiles):
        for k0 in range(0, (t + 1) * P, CHUNK):
            w = min(CHUNK, (t + 1) * P - k0)
            n = 4 if w == P else 2 if w == 2 * P else 1
            units += [(t, k0, w, tuple(range(j, j + n)), k0 + w == (t + 1) * P) for j in range(0, HPG, n)]
    return units


def score_steps(tiles):
    return [(c, kt, max(kt * P, c * CHUNK), kt == TPC * (c + 1) - 1)
            for c in range(tiles // TPC) for kt in range(TPC * (c + 1))]


def attention_order(b, groups, tiles, beside):
    chunks = tiles // TPC
    units, steps = max_units(tiles), score_steps(tiles)
    blocks = [(0, 0), (0, 1), (1, 0), (2, 0), (1, 1), (3, 0), (2, 1), (3, 1)]
    todo = [(g, u) for g, c in blocks for u, unit in enumerate(units) if unit[0] // TPC == c]
    at = [(g, s) for g, c in blocks for s, step in enumerate(steps) if step[0] == c]
    first_step = [at.index((g, min(s for s, step in enumerate(steps) if step[0] == c))) for g, c in blocks]
    needed = [sum(units[u][0] // TPC == c for u in range(len(units))) for _, c in blocks]
    needed = [sum(needed[:i + 1]) for i in range(len(blocks))]
    course = [(0, needed[0] + 6), (first_step[1], needed[1] + 8), (first_step[-1] - 3, needed[-1])]
    order, issued, due = [], 0, []

    def issue_max(upto):
        nonlocal issued
        if issued == len(todo) and due:
            order.append(("rows", b, *due.pop(0)[1:]))
        while issued < min(upto, len(todo)):
            g, u = todo[issued]
            order.append(("max", b, g, u))
            issued += 1
            if issued in needed:
                g, c = blocks[needed.index(issued)]
                order.append(("split", b, g, c))
                due.append((issued + 3, g, c))
            while due and issued >= due[0][0]:
                order.append(("rows", b, *due.pop(0)[1:]))

    def target(k):
        for (k0, n0), (k1, n1) in zip(course, course[1:]):
            if k < k1:
                return n0 + (n1 - n0) * (k - k0) / (k1 - k0)
        return len(todo)

    issue_max(course[0][1])
    opening, order = order, []
    for k in range(len(at) + 3):
        for j in range(HPG):
            if k < len(at):
                if j == 0 and k in first_step:
                    n = first_step.index(k)
                    issue_max(needed[n])
                    while due and blocks.index(due[0][1:]) <= n:
                        order.append(("rows", b, *due.pop(0)[1:]))
                order.append(("score", b, *at[k], j))
            issue_max(int(target(k + (j + 1) / HPG)))
            for behind, when, kind in ((2, 0, "drain"), (3, 1, "turn")):
                if j == when and 0 <= k - behind < len(at) and steps[at[k - behind][1]][3]:
                    order.append((kind, b, at[k - behind][0], steps[at[k - behind][1]][0]))
            more = beside.get(k, [])
            order += more[j * len(more) // HPG:(j + 1) * len(more) // HPG]
        if 0 < k <= len(at):
            order.append(("value", b, *at[k - 1]))
            g, s = at[k - 1]
            if s == len(steps) - 1 and g + STACKS < groups:
                order += [("stack", b, g + STACKS, c) for c in range(chunks)]
    return opening, order


def woven(*lists):
    at = sorted(((i + 0.5) / len(l), n, i) for n, l in enumerate(lists) for i in range(len(l)))
    return [lists[n][i] for _, n, i in at]


def program_order(batches, groups, tiles, parts):
    C = tiles // TPC
    ks, pairs = range(parts), range(0, tiles, 2)

    def chunk_tiles(c):
        return range(c * TPC, (c + 1) * TPC)

    def begin(b, c):
        return ([("xt", b, c, k) for k in ks] + [("qk", b, m, c, w) for m in ks for w in range(2)]
                + [("stack", b, 0, c)])

    def residual(b, c):
        return [("ot", b, c, k) for k in ks] + [
            ("r1", b, t) for t in pairs if t in chunk_tiles(c)] + [("ln2", b, c * TPC, TPC)]

    def mixture(b, c):
        return ([("x1t", b, c, k) for k in ks], [("h", b, c, k) for k in ks] + [("lg", b, c), ("weigh", b, c)])

    def maps(b, c):
        ts = chunk_tiles(c)
        o = [[("vx", b, t)] * (t in ts) + [("avt", b, t - 1)] * (t - 1 in ts) + [("u", b, t - 2)] * (t - 2 in ts)
             for t in range(ts[0], ts[-1] + 3)]
        return [e for part in o for e in part]

    half = len(pairs) // 2
    vs = [[("v", b, t) for t in pairs] for b in range(batches)]
    third = [[("ln3", b, c * TPC, TPC) for c in range(C)] for b in range(batches)]
    order = ([("load", 0)] + [("ln1", 0, c * TPC, TPC) for c in range(C)] + [("bo", 0)] + begin(0, 0) + begin(0, 1)[:parts])
    for b in range(batches):
        nb = b + 1
        res = [residual(b, c) for c in range(C)]
        mix = [mixture(b, c) for c in range(C)]
        m = [maps(b, c) for c in range(C)]
        beside = {35: res[0][:parts], 36: res[0][parts:parts + 1], 37: res[0][parts + 1:], 41: mix[0][0], 42: mix[0][1][:parts], 43: mix[0][1][parts:], 44: [("alpha", b, 0)] + m[0][:1], 45: m[0][1:2],
                  46: m[0][2:4], 47: m[0][4:6], 48: m[0][6:7], 49: m[0][7:8], 50: m[0][8:9]}
        if nb < batches:
            beside[30] = [("early", nb)]
            beside[38] = [("ln1", nb, 0, TPC)]
            beside[43] += [("ln1", nb, TPC, TPC)]
        if b == 0:
            beside[0], beside[1] = vs[0][1:3], vs[0][3:]
        opening, rest = attention_order(b, groups, tiles, beside)
        stacks = [("stack", b, g, c) for g in range(1, STACKS) for c in range(C)]
        qks = begin(b, 1)[parts:]
        if b == 0:
            order += qks + woven(opening, vs[0][:1]) + stacks
        else:
            order += qks[:3] + woven(qks[3:-1], before[:5], opening[:5]) + qks[-1:]
            order += woven(before[5:], opening[5:], vs[b][:1]) + third[b - 1][1:] + vs[b][1:] + stacks
        order += rest
        turned, mixed = mix[1]
        ot, (r4, r6, n) = res[1][:parts], res[1][parts:]
        if nb < batches:
            first, second = begin(nb, 0), begin(nb, 1)
            before = m[1]
            order += ot + first[:parts] + [r4, r6, n] + first[parts:parts + 2] + m[0][9:]
            order += [("load", nb), ("bo", nb)] + turned + first[parts + 2:parts + 3] + mixed[:parts] + first[parts + 3:]
            order += mixed[parts:] + second[:parts] + [("alpha", b, 1)] + third[b][:1]
        else:
            order += ot + [r4, r6, n] + m[0][9:] + turned + mixed
            order += [("alpha", b, 1)] + m[1][:2] + third[b][:1] + m[1][2:-3] + [("ln3", b, TPC, 2)] + m[1][-3:] + [("ln3", b, TPC + 2, 2)]
    return order


def block_kernel(nc, x, vecs, rows, wq, wk, wv, wo, w1, w2, vt, ut, out):
    NB, S, D = x.shape
    T = S // P
    C = S // CHUNK
    KC = D // P
    E = w2.shape[1]
    ER = vt.shape[1]
    RC = ER // P
    G = HEADS // HPG
    PAIRS = HPG // 2
    units, steps = max_units(T), score_steps(T)
    U, ST = len(units), len(steps)
    order = program_order(NB, G, T, KC)

    x_v = x.rearrange("b (t p) d -> b p t d", p=P)
    out_v = out.rearrange("b (t p) d -> b p t d", p=P)

    with ExitStack() as ctx:
        def sb(name, shape, dt=F32):
            return ctx.enter_context(nc.sbuf_tensor(name, shape, dt))

        def sem(name):
            return ctx.enter_context(nc.semaphore(name))

        w_qk = sb("w_qk", [P, KC, 2, D])
        w_v = sb("w_v", [P, KC, D])
        w_o = sb("w_o", [P, KC, D])
        w_1 = sb("w_1", [P, KC, D])
        w_2 = sb("w_2", [P, KC, E])
        v_t = sb("v_t", [P, KC, ER])
        u_t = sb("u_t", [P, RC, D])
        cols = sb("cols", [P, 5, KC])
        flat = sb("flat", [P, 2 * D + E])
        ident = sb("ident", [P, P])
        ident_b = sb("ident_b", [P, P], BF16)
        mask = sb("mask", [P, P], BF16)

        x_in = sb("x_in", [P, T, D])
        x1 = sb("x1", [P, T, D])
        qk = sb("qk", [P, 2, 2, C, KC, CHUNK])
        va = sb("va", [P, T, HEADS, VW])
        stq = [sb(f"stq{i}", [P, C, HPG, CHUNK], F32R) for i in range(STACKS)]
        stk = [sb(f"stk{i}", [P, C, PAIRS, CHUNK], F32R) for i in range(STACKS)]
        pr = [sb(f"pr{i}", [P, HPG, CHUNK]) for i in range(PROBS)]
        mx = sb("mx", [P, 2, C, C, HPG, TPC])
        mhl = sb("mhl", [P, 2, 2, HPG, TPC], F32R)
        mrow = sb("mrow", [2 * HPG * TPC, 2, P], F32R)
        av_raw = sb("av_raw", [P, 2, CHUNK])
        rs = sb("rs", [P, TPC, HPG])
        st6 = sb("st6", [P, T, 6])
        mv = sb("mv", [P, T, 2])
        nv = sb("nv", [P, 4, TPC])
        rstd = sb("rstd", [P, T])
        lg = sb("lg", [P, C, TPC, E])
        le = sb("le", [P, C, TPC, E])
        sm = sb("sm", [P, C, TPC])
        alpha = sb("alpha", [P, C, TPC, E])

        o_t = h_t = sb("o_t", [P, KC, CHUNK])
        x1_t = sb("x1_t", [P, KC, CHUNK])
        avx = sb("avx", [P, 2, ER])
        avt = sb("avt", [P, 2, ER])

        o_sb = y = x1
        early_x, early_xh = ([qk[:, w, w, c].rearrange("p m (t d) -> p (m t) d", d=D) for c in range(C)] for w in range(2))
        xt = pr[2][:].rearrange("p (c k) s -> p c k s", c=C)

        ps = ctx.enter_context(nc.psum_tensor("ps", [P, 8, CHUNK], F32))
        values_bank = ps[:, DVE_RING + ACT_RING, :]

        s_cols = sem("s_cols")
        s_flat = sem("s_flat")
        s_w = {n: sem(f"s_w_{n}") for n in ("qk", "v", "o", "1", "2", "vt", "ut")}
        s_early = sem("s_early")
        s_x = [sem(f"s_x{i}") for i in range(T // 2)]
        s_ident = sem("s_ident")
        s_mask = sem("s_mask")
        s_stack_init = sem("s_stack_init")
        s_minus = sem("s_minus")
        s_ones = sem("s_ones")
        s_bo = sem("s_bo")
        s_dve = sem("s_dve")
        s_xh = sem("s_xh")
        s_act_full = sem("s_act_full")
        s_act_free = sem("s_act_free")
        s_dve_full = sem("s_dve_full")
        s_dve_free = sem("s_dve_free")
        s_high = sem("s_high")
        s_stack = [[sem(f"s_stack{i}_{c}") for c in range(C)] for i in range(STACKS)]
        s_split = sem("s_split")
        s_rows = [sem(f"s_rows{i}") for i in range(2)]
        s_causal = sem("s_causal")
        s_value = sem("s_value")
        s_drain = sem("s_drain")
        s_x1 = sem("s_x1_done")
        s_logits = sem("s_logits")
        s_weighed = sem("s_weighed")
        s_y = sem("s_y")
        s_out = sem("s_out")

        def count(*kinds):
            return {ev: n + 1 for n, ev in enumerate(e for e in order if e[0] in kinds)}

        n_act = count("xt", "score", "ot", "x1t", "h", "avt")
        n_dve = count("qk", "v", "max", "rows", "turn", "r1", "lg", "vx", "u")
        n_high = count("qk")
        n_ln1, n_ln2, n_ln3, n_weigh = count("ln1"), count("ln2"), count("ln3"), count("weigh")
        n_logits = count("lg")
        n_split, n_rows = count("split"), count("rows")
        n_value, n_drain = count("value"), count("drain")
        on_diagonal = [s for s, (c, kt, q0, _) in enumerate(steps) if q0 == kt * P]
        n_causal = {ev: n + 1 for n, ev in enumerate(e for e in order if e[0] == "value" and e[3] in on_diagonal)}
        LOADS = 16 * 6

        def act_bank(ev):
            return ps[:, DVE_RING + (n_act[ev] - 1) % ACT_RING, :]

        def dve_bank(ev):
            return ps[:, (n_dve[ev] - 1) % DVE_RING, :]

        def probs(b, g, s):
            return pr[(n_value["value", b, g, s] - 1) % PROBS]

        def xh(b, c):
            return early_xh[c] if b else pr[0][:, 2 * c:2 * c + 2].rearrange("p h (t d) -> p (h t) d", d=D)

        def stored(b):
            return sum(ev[1] < b for ev in n_ln3)

        def stack_of(b, g):
            return (b * G + g) % STACKS

        def last_step(c):
            return [s for s in range(ST) if steps[s][0] == c][-1]

        def span(c):
            return slice(c * CHUNK, (c + 1) * CHUNK)

        def tile(t):
            return slice(t * P, (t + 1) * P)

        block = ctx.enter_context(nc.Block())

        @block.sync
        def _(sp):
            def weight(dst, src, name):
                sp.dma_start(dst, src.rearrange("(k p) n -> p k n", p=P)).then_inc(s_w[name], 16)

            for ev in order:
                kind, b = ev[:2]
                if kind == "load":
                    for i in range(T // 2):
                        if b and i == 0:
                            sp.wait_ge(s_x1, n_ln2["ln2", b - 1, (C - 1) * TPC, TPC])
                        sp.dma_start(x_in[:, 2 * i:2 * i + 2, :], x_v[b, :, 2 * i:2 * i + 2, :]).then_inc(s_x[i], 16)
                        if b == 0 and i == 1:
                            sp.dma_start(cols[:], vecs.rearrange("p (v k) -> p v k", v=5)).then_inc(s_cols, 16)
                            weight(w_qk[:, :, 0, :], wq, "qk")
                            weight(w_qk[:, :, 1, :], wk, "qk")
                    if b == 0:
                        sp.dma_start(flat[:], rows.partition_broadcast(P)).then_inc(s_flat, 16)
                        weight(w_v[:], wv, "v")
                if kind == "early":
                    for c in range(C):
                        sp.wait_ge(s_stack[stack_of(b - 1, G - 1)][c], LOADS * ((b * G - 1) // STACKS + 1))
                    for c in range(C):
                        sp.dma_start(early_x[c], x_v[b, :, c * TPC:(c + 1) * TPC, :]).then_inc(s_early, 16)
                if kind == "stack":
                    _, _, g, c = ev
                    sp.wait_ge(s_dve_free, n_dve["qk", b, KC - 1, c, 1])
                    n = b * G + g
                    if n < STACKS:
                        sp.wait_ge(s_stack_init, n + 1)
                    else:
                        sp.wait_ge(s_value, n_value["value", *divmod(n - STACKS, G), ST - 1])
                    q, k = stq[stack_of(b, g)], stk[stack_of(b, g)]
                    two, one = slice(0, ROWS * 2 // 3), slice(ROWS * 2 // 3, ROWS)
                    heads = slice(2 * g * DH, 2 * (g + 1) * DH)
                    loads = [(k[two, c], qk[heads, 1, :, c]), (k[one, c], qk[heads, 1, 0, c])]
                    for i in range(2):
                        head = slice((2 * g + i) * DH, (2 * g + i + 1) * DH)
                        high = qk[head, 0, 0, c].rearrange("p m s -> p (m s)").unsqueeze(1)
                        loads += [(q[2 * i * DH:2 * (i + 1) * DH, c, 2 * i:2 * i + 2], high.to_broadcast([DH, 2, KC * CHUNK])),
                                  (q[one.start + i * DH:one.start + (i + 1) * DH, c, 2 * i:2 * i + 2], qk[head, 0, 1, c])]
                    for dst, src in loads:
                        sp.dma_start(dst.bitcast(F32), src).then_inc(s_stack[stack_of(b, g)][c], 16)
                    if n == 0 and c == C - 1:
                        weight(w_o[:], wo, "o")
                        weight(w_1[:], w1, "1")
                        weight(w_2[:], w2, "2")
                        weight(v_t[:], vt, "vt")
                        weight(u_t[:], ut, "ut")
                if kind == "rows":
                    _, _, g, c = ev
                    sp.wait_ge(s_dve_free, n_dve[ev])
                    sp.dma_start(stq[stack_of(b, g)][ROWS:ROWS + 2, c].bitcast(F32),
                                 mrow[:, c, :].bitcast(F32)).then_inc(s_rows[c], 16)
                if kind == "ln3":
                    _, _, t, n = ev
                    sp.wait_ge(s_y, n_ln3[ev])
                    sp.dma_start(out_v[b, :, t:t + n, :], y[:, t:t + n, :]).then_inc(s_out, 16)
            sp.wait_ge(s_out, 16 * stored(NB))

        @block.gpsimd
        def _(pool):
            pool.memset(ident[:], 0.0).then_inc(s_ident, 1)
            pool.memset(stq[0][0:ROWS].bitcast(F32), 0.0).then_inc(s_stack_init, 1)
            pool.wait_ge(s_ident, 1)
            pool.affine_select(out=ident[:], in_=ident[:], compare_op=ALU.not_equal, fill=1.0, base=0,
                               pattern=[[-1, P]], channel_multiplier=1).then_inc(s_ident, 1)
            pool.memset(ident_b[:], 0.0).then_inc(s_mask, 1)
            pool.memset(mask[:], 0.0).then_inc(s_mask, 1)
            pool.wait_ge(s_mask, 2)
            pool.affine_select(out=ident_b[:], in_=ident_b[:], compare_op=ALU.not_equal, fill=1.0, base=0,
                               pattern=[[-1, P]], channel_multiplier=1).then_inc(s_mask, 1)
            pool.affine_select(out=mask[:], in_=mask[:], compare_op=ALU.is_ge, fill=MASKED, base=0,
                               pattern=[[-1, P]], channel_multiplier=1).then_inc(s_mask, 1)
            pool.memset(va[:, :, :, DH:], 1.0).then_inc(s_ones, 1)
            for i in range(1, STACKS):
                pool.memset(stq[i][0:ROWS].bitcast(F32), 0.0).then_inc(s_stack_init, 1)
            pool.wait_ge(s_stack_init, STACKS)
            for i in range(STACKS):
                pool.memset(stk[i][ROWS:ROWS + 2].bitcast(F32), -1.0).then_inc(s_minus, 1)
                pool.wait_ge(s_minus, i + 1)
            for ev in order:
                kind, b = ev[:2]
                if kind == "bo":
                    pool.wait_ge(s_flat, 16)
                    for t in range(T):
                        if t % 2 == 0:
                            pool.wait_ge(s_x[t // 2], 16 * (b + 1))
                        if b == 0 and t % TPC == 0:
                            pool.wait_ge(s_xh, t // TPC + 1)
                        pool.tensor_tensor(x_in[:, t, :], x_in[:, t, :], flat[:, D:2 * D], ALU.add).then_inc(s_bo, 1)
                if kind == "value" and ev in n_causal:
                    _, _, g, s = ev
                    q0 = steps[s][2]
                    blk = probs(b, g, s)[:, :, q0 % CHUNK:q0 % CHUNK + P]
                    pool.wait_ge(s_act_free, n_act["score", b, g, s, HPG - 1])
                    pool.affine_select(out=blk, in_=blk, compare_op=ALU.is_ge, fill=0.0, base=0,
                                       pattern=[[0, HPG], [1, P]], channel_multiplier=-1).then_inc(s_causal, 1)

        @block.scalar
        def _(act):
            act.wait_ge(s_cols, 16)
            nc.scalar.activation(le[:, 0, 0, 0:1], cols[:, 0, 0:1], ACT.Exp)
            for ev in order:
                kind, b = ev[:2]
                if kind in ("xt", "ot", "x1t", "h"):
                    _, _, c, k = ev
                    act.wait_ge(s_act_full, n_act[ev])
                    if kind == "xt":
                        ins = nc.scalar.activation(xt[:, c, k, :], act_bank(ev), ACT.Identity,
                                                   scale=cols[:, 0, k:k + 1], bias=cols[:, 1, k:k + 1])
                    elif kind == "h":
                        ins = nc.scalar.activation(h_t[:, k, :], act_bank(ev), ACT.Relu, bias=cols[:, 4, k:k + 1])
                    else:
                        ins = nc.scalar.activation((o_t if kind == "ot" else x1_t)[:, k, :], act_bank(ev), ACT.Copy)
                    ins.then_inc(s_act_free, 1)
                if kind == "qk":
                    _, _, m, c, w = ev
                    act.wait_ge(s_dve_full, n_dve[ev])
                    nc.scalar.activation(qk[:, w, 0, c, m].bitcast(F32R), dve_bank(ev),
                                         ACT.Identity, bias=cols[:, 2 + w, m:m + 1]).then_inc(s_high, 1)
                if kind == "score":
                    _, _, g, s, j = ev
                    c, kt, q0, _ = steps[s]
                    n = n_value["value", b, g, s]
                    if j == 0 and n > PROBS:
                        act.wait_ge(s_value, n - PROBS)
                    act.wait_ge(s_act_full, n_act[ev])
                    nc.scalar.activation(probs(b, g, s)[:, j, q0 - c * CHUNK:], act_bank(ev)[:, q0 - c * CHUNK:],
                                         ACT.Exp, scale=DH ** -0.5).then_inc(s_act_free, 1)
                if kind == "drain":
                    _, _, g, c = ev
                    act.wait_ge(s_value, n_value["value", b, g, last_step(c)])
                    n = n_drain[ev]
                    if n > 2:
                        before = [e for e in order if e[0] == "drain"][n - 3]
                        act.wait_ge(s_dve_full, n_dve["turn", *before[1:]])
                    nc.scalar.activation(av_raw[:, n % 2, :], values_bank, ACT.Copy).then_inc(s_drain, 1)
                if kind == "weigh":
                    c = ev[2]
                    act.wait_ge(s_logits, n_logits["lg", b, c])
                    nc.scalar.activation(le[:, c], lg[:, c], ACT.Exp).then_inc(s_weighed, 1)
                if kind == "avt":
                    t = ev[2]
                    act.wait_ge(s_act_full, n_act[ev])
                    if t >= 2:
                        act.wait_ge(s_dve_full, n_dve["u", b, t - 2])
                    nc.scalar.activation(avt[:, t % 2, :], act_bank(ev), ACT.Copy).then_inc(s_act_free, 1)

        @block.vector
        def _(dve):
            done = [0]

            def link(ins):
                done[0] += 1
                ins.then_inc(s_dve, 1)
                dve.wait_ge(s_dve, done[0])

            def make_rstd(ts):
                v, i, yy, t = (nv[:, n, :len(ts)] for n in range(4))
                span_ = slice(ts[0], ts[-1] + 1)
                link(nc.vector.tensor_scalar(v, mv[:, span_, 1], LN_EPS, None, ALU.add))
                link(nc.vector.tensor_scalar(i.bitcast(I32), v.bitcast(I32), 1, None, ALU.logical_shift_right))
                link(nc.vector.tensor_scalar(yy.bitcast(I32), i.bitcast(I32), -1.0, RSQRT_MAGIC, ALU.mult, ALU.add))
                for step in range(3):
                    link(nc.vector.tensor_tensor(t, yy, yy, ALU.mult))
                    link(nc.vector.scalar_tensor_tensor(i, t, -0.5, v, ALU.mult, ALU.mult))
                    dst = rstd[:, span_] if step == 2 else yy
                    link(nc.vector.scalar_tensor_tensor(dst, i, 1.5, yy, ALU.add, ALU.mult))

            def layer_norm(ts, dst, src, sem_):
                for t in ts:
                    ins = nc.vector.bn_stats(st6[:, t, :], src[:, t - ts[0], :])
                link(ins)
                for t in ts:
                    ins = nc.vector.bn_aggr(mv[:, t, :], st6[:, t, :])
                link(ins)
                make_rstd(ts)
                for t in ts:
                    ins = nc.vector.tensor_scalar(dst[:, t - ts[0], :], src[:, t - ts[0], :], mv[:, t, 0:1], rstd[:, t:t + 1],
                                                  ALU.subtract, ALU.mult)
                ins.then_inc(sem_, 1)

            for ev in order:
                kind, b = ev[:2]
                if kind == "ln1":
                    _, _, t, n = ev
                    if b == 0:
                        for i in range(t // 2, (t + n) // 2):
                            dve.wait_ge(s_x[i], 16)
                    else:
                        dve.wait_ge(s_early, 16 * C * b)
                    c = t // TPC
                    layer_norm(range(t, t + n), xh(b, c), early_x[c] if b else x_in[:, t:t + n], s_xh)
                if kind == "qk":
                    _, _, m, c, w = ev
                    if n_high[ev] == 1:
                        dve.wait_ge(s_cols, 16)
                        dve.wait_ge(s_flat, 16)
                    dve.wait_ge(s_high, n_high[ev])
                    nc.vector.scalar_tensor_tensor(
                        qk[:, w, 1, c, m].bitcast(F32R), dve_bank(ev), cols[:, 2 + w, m:m + 1],
                        qk[:, w, 0, c, m], ALU.add, ALU.subtract).then_inc(s_dve_free, 1)
                if kind == "v":
                    t = ev[2]
                    dve.wait_ge(s_dve_full, n_dve[ev])
                    nc.vector.tensor_tensor(
                        va[:, t:t + 2, :, 0:DH],
                        dve_bank(ev).rearrange("p (t h d) -> p t h d", t=2, h=HEADS),
                        flat[:, 0:D].rearrange("p (h d) -> p h d", h=HEADS).unsqueeze(1).to_broadcast([P, 2, HEADS, DH]),
                        ALU.add).then_inc(s_dve_free, 1)
                if kind == "max":
                    _, _, g, u = ev
                    t, k0, w, heads, _ = units[u]
                    dve.wait_ge(s_dve_full, n_dve[ev])
                    if t % TPC == 0 and k0 == 0 and heads[0] == 0 and b * G + g >= 2:
                        dve.wait_ge(s_split, n_split["split", *divmod(b * G + g - 2, G), t // TPC])
                    dst = mx[:, g % 2, t // TPC, k0 // CHUNK, heads[0]:heads[-1] + 1, t % TPC]
                    src = dve_bank(ev)[:, 0:len(heads) * w].rearrange("p (h k) -> p h k", k=w)
                    nc.vector.tensor_reduce(dst, src, AX.X, ALU.max).then_inc(s_dve_free, 1)
                    last_max = n_dve[ev]
                if kind == "split":
                    _, _, g, c = ev
                    dve.wait_ge(s_dve_free, last_max)
                    whole = mx[:, g % 2, c, 0]
                    if c:
                        link(nc.vector.tensor_tensor(whole, mx[:, g % 2, c, 0], mx[:, g % 2, c, 1], ALU.max))
                    if b * G + g:
                        dve.wait_ge(s_dve_full, n_dve["rows", *divmod(b * G + g - 1, G), c])
                    link(nc.vector.tensor_copy(mhl[:, c, 0], whole))
                    nc.vector.tensor_tensor(mhl[:, c, 1], whole, mhl[:, c, 0].bitcast(F32),
                                            ALU.subtract).then_inc(s_split, 1)
                if kind == "rows":
                    _, _, g, c = ev
                    dve.wait_ge(s_dve_full, n_dve[ev])
                    if b * G + g:
                        dve.wait_ge(s_rows[c], 16 * (b * G + g))
                    nc.vector.tensor_copy(mrow[:, c, :], dve_bank(ev)[0:2 * HPG * TPC, 0:P]).then_inc(s_dve_free, 1)
                if kind == "turn":
                    _, _, g, c = ev
                    dve.wait_ge(s_dve_full, n_dve[ev])
                    if b and g == 0 and c == 0:
                        dve.wait_ge(s_out, 16 * stored(b))
                    o4 = dve_bank(ev).rearrange("p (t h v) -> p t h v", t=TPC, h=HPG)
                    link(nc.vector.reciprocal(rs[:], o4[:, :, :, DH]))
                    nc.vector.tensor_tensor(
                        o_sb[:, c * TPC:(c + 1) * TPC, g * HPG * DH:(g + 1) * HPG * DH].rearrange(
                            "p t (h d) -> p t h d", h=HPG),
                        o4[:, :, :, 0:DH], rs[:].unsqueeze(3).to_broadcast([P, TPC, HPG, DH]),
                        ALU.mult).then_inc(s_dve_free, 1)
                if kind == "r1":
                    t = ev[2]
                    dve.wait_ge(s_dve_full, n_dve[ev])
                    dve.wait_ge(s_bo, b * T + t + 2)
                    nc.vector.tensor_tensor(x_in[:, t:t + 2, :], dve_bank(ev).rearrange("p (t d) -> p t d", t=2),
                                            x_in[:, t:t + 2, :], ALU.add).then_inc(s_dve_free, 1)
                    dve.wait_ge(s_dve_free, n_dve[ev])
                if kind == "ln2":
                    layer_norm(range(ev[2], ev[2] + ev[3]), x1[:, ev[2]:ev[2] + ev[3]], x_in[:, ev[2]:ev[2] + ev[3]], s_x1)
                if kind == "lg":
                    c = ev[2]
                    dve.wait_ge(s_dve_full, n_dve[ev])
                    b2 = flat[:, 2 * D:].unsqueeze(1).to_broadcast([P, TPC, E])
                    nc.vector.tensor_tensor(lg[:, c], dve_bank(ev)[:, 0:TPC * E].rearrange("p (t e) -> p t e", t=TPC), b2,
                                            ALU.add).then_inc(s_dve_free, 1)
                    dve.wait_ge(s_dve_free, n_dve[ev])
                    link(nc.vector.tensor_reduce(sm[:, c], lg[:, c], AX.X, ALU.max))
                    nc.vector.tensor_tensor(lg[:, c], lg[:, c], sm[:, c].unsqueeze(2).to_broadcast([P, TPC, E]),
                                            ALU.subtract).then_inc(s_logits, 1)
                if kind == "alpha":
                    c = ev[2]
                    dve.wait_ge(s_weighed, n_weigh["weigh", b, c])
                    link(nc.vector.tensor_reduce(sm[:, c], le[:, c], AX.X, ALU.add))
                    link(nc.vector.reciprocal(sm[:, c], sm[:, c]))
                    link(nc.vector.tensor_tensor(alpha[:, c], le[:, c], sm[:, c].unsqueeze(2).to_broadcast([P, TPC, E]),
                                                 ALU.mult))
                if kind == "vx":
                    t = ev[2]
                    dve.wait_ge(s_dve_full, n_dve[ev])
                    if t >= 2:
                        dve.wait_ge(s_act_full, n_act["avt", b, t - 2])
                    nc.vector.tensor_tensor(
                        avx[:, t % 2, :].rearrange("p (e r) -> p e r", e=E),
                        dve_bank(ev).rearrange("p (e r) -> p e r", e=E),
                        alpha[:, t // TPC, t % TPC, :].unsqueeze(2).to_broadcast([P, E, ER // E]),
                        ALU.mult).then_inc(s_dve_free, 1)
                if kind == "u":
                    t = ev[2]
                    dve.wait_ge(s_dve_full, n_dve[ev])
                    nc.vector.tensor_tensor(x1[:, t, :], dve_bank(ev)[:, 0:D], x1[:, t, :], ALU.add).then_inc(s_dve_free, 1)
                if kind == "ln3":
                    dve.wait_ge(s_dve_free, n_dve["u", b, ev[2] + ev[3] - 1])
                    layer_norm(range(ev[2], ev[2] + ev[3]), y[:, ev[2]:ev[2] + ev[3]], x1[:, ev[2]:ev[2] + ev[3]], s_y)

        @block.tensor
        def _(pe):
            def take_act(ev):
                if n_act[ev] > ACT_RING:
                    pe.wait_ge(s_act_free, n_act[ev] - ACT_RING)
                return act_bank(ev)

            def take_dve(ev):
                if n_dve[ev] > DVE_RING:
                    pe.wait_ge(s_dve_free, n_dve[ev] - DVE_RING)
                return dve_bank(ev)

            def weights(name, b, n=16):
                if b == 0:
                    pe.wait_ge(s_w[name], n)

            def turn(bank, src, k):
                for i in range(TPC):
                    last = nc.tensor.transpose(bank[:, tile(i)], src[:, i, tile(k)], ident[:])
                return last

            def product(out_, lhs, rhs, n):
                for k in range(n):
                    last = nc.tensor.matmul(out_, lhs(k), rhs(k), start=(k == 0), stop=(k == n - 1))
                return last

            pe.wait_ge(s_ident, 2)
            for ev in order:
                kind, b = ev[:2]
                if kind in ("xt", "ot", "x1t"):
                    _, _, c, k = ev
                    bank = take_act(ev)
                    if kind == "xt":
                        pe.wait_ge(s_xh, n_ln1["ln1", b, c * TPC, TPC])
                        src = xh(b, c)
                    if kind == "ot":
                        pe.wait_ge(s_dve_free, n_dve["turn", b, G - 1, c])
                        src = o_sb[:, c * TPC:(c + 1) * TPC]
                    if kind == "x1t":
                        pe.wait_ge(s_x1, n_ln2["ln2", b, c * TPC, TPC])
                        src = x1[:, c * TPC:(c + 1) * TPC]
                    turn(bank, src, k).then_inc(s_act_full, 1)
                if kind == "qk":
                    _, _, m, c, w = ev
                    bank = take_dve(ev)
                    weights("qk", b, 32)
                    pe.wait_ge(s_act_free, n_act["xt", b, c, KC - 1])
                    product(bank, lambda k: w_qk[:, k, w, tile(m)], lambda k: xt[:, c, k, :], KC).then_inc(s_dve_full, 1)
                if kind == "v":
                    t = ev[2]
                    bank = take_dve(ev)
                    weights("v", b)
                    for i in range(2):
                        c, n = divmod(t + i, TPC)
                        last = product(bank[:, i * D:(i + 1) * D], lambda k: xt[:, c, k, tile(n)], lambda k: w_v[:, k, :], KC)
                    last.then_inc(s_dve_full, 1)
                if kind == "max":
                    _, _, g, u = ev
                    t, k0, w, heads, diagonal = units[u]
                    q, k = stq[stack_of(b, g)], stk[stack_of(b, g)]
                    if t % TPC == 0 and k0 == 0 and heads[0] == 0:
                        pe.wait_ge(s_stack[stack_of(b, g)][t // TPC], LOADS * ((b * G + g) // STACKS + 1))
                        if b == 0 and g == 0:
                            pe.wait_ge(s_mask, 4)
                    bank = take_dve(ev)
                    for i, j in enumerate(heads):
                        last = nc.tensor.matmul(bank[:, i * w:(i + 1) * w], q[0:ROWS, t // TPC, j, tile(t % TPC)],
                                                k[0:ROWS, k0 // CHUNK, j % 2, 0:w], start=True, stop=not diagonal)
                        if diagonal:
                            last = nc.tensor.matmul(bank[:, (i + 1) * w - P:(i + 1) * w], ident_b[:], mask[:],
                                                    start=False, stop=True)
                    last.then_inc(s_dve_full, 1)
                if kind == "rows":
                    _, _, g, c = ev
                    pe.wait_ge(s_split, n_split["split", b, g, c])
                    nc.tensor.transpose(take_dve(ev)[0:2 * HPG * TPC, 0:P],
                                        mhl[:, c].rearrange("p a h t -> p (a h t)").bitcast(F32),
                                        ident[:]).then_inc(s_dve_full, 1)
                if kind == "score":
                    _, _, g, s, j = ev
                    c, kt, q0, _ = steps[s]
                    if kt == 0 and j == 0:
                        if b == g == c == 0:
                            pe.wait_ge(s_minus, STACKS)
                        pe.wait_ge(s_rows[c], 16 * (b * G + g + 1))
                    bank = take_act(ev)
                    nc.tensor.matmul(bank[:, q0 - c * CHUNK:], stk[stack_of(b, g)][0:ROWS + 2, kt // TPC, j % 2, tile(kt % TPC)],
                                     stq[stack_of(b, g)][0:ROWS + 2, c, j, q0 - c * CHUNK:],
                                     start=True, stop=True).then_inc(s_act_full, 1)
                if kind == "value":
                    _, _, g, s = ev
                    c, kt, q0, ends = steps[s]
                    if ev in n_causal:
                        pe.wait_ge(s_causal, n_causal[ev])
                    else:
                        pe.wait_ge(s_act_free, n_act["score", b, g, s, HPG - 1])
                    if n_value[ev] == 1:
                        pe.wait_ge(s_ones, 1)
                    if g == 0:
                        pe.wait_ge(s_dve_free, n_dve["v", b, kt // 2 * 2])
                    if kt == 0:
                        if n_drain["drain", b, g, c] > 1:
                            pe.wait_ge(s_drain, n_drain["drain", b, g, c] - 1)
                    for j in range(HPG):
                        last = nc.tensor.matmul(values_bank[j * VW:(j + 1) * VW, q0 - c * CHUNK:],
                                                va[:, kt, g * HPG + j, :], probs(b, g, s)[:, j, q0 - c * CHUNK:],
                                                start=(kt == 0), stop=ends)
                    last.then_inc(s_value, 1)
                if kind == "turn":
                    _, _, g, c = ev
                    n = n_drain["drain", b, g, c]
                    pe.wait_ge(s_drain, n)
                    bank = take_dve(ev)
                    for i in range(TPC):
                        last = nc.tensor.transpose(bank[:, tile(i)], av_raw[:, n % 2, tile(i)], ident[:])
                    last.then_inc(s_dve_full, 1)
                if kind == "r1":
                    t = ev[2]
                    bank = take_dve(ev)
                    weights("o", b)
                    pe.wait_ge(s_act_free, n_act["ot", b, t // TPC, KC - 1])
                    for i in range(2):
                        last = product(bank[:, i * D:(i + 1) * D], lambda k: o_t[:, k, tile((t + i) % TPC)], lambda k: w_o[:, k, :], KC)
                    last.then_inc(s_dve_full, 1)
                if kind == "h":
                    _, _, c, m = ev
                    bank = take_act(ev)
                    weights("1", b)
                    pe.wait_ge(s_act_free, n_act["x1t", b, c, KC - 1])
                    product(bank, lambda k: w_1[:, k, tile(m)], lambda k: x1_t[:, k, :], KC).then_inc(s_act_full, 1)
                if kind == "lg":
                    c = ev[2]
                    bank = take_dve(ev)
                    weights("2", b)
                    pe.wait_ge(s_act_free, n_act["h", b, c, KC - 1])
                    for i in range(TPC):
                        last = product(bank[:, i * E:(i + 1) * E], lambda k: h_t[:, k, tile(i)],
                                       lambda k: w_2[:, k, :], KC)
                    last.then_inc(s_dve_full, 1)
                if kind == "vx":
                    t = ev[2]
                    bank = take_dve(ev)
                    weights("vt", b)
                    product(bank, lambda k: x1_t[:, k, tile(t % TPC)], lambda k: v_t[:, k, :], KC).then_inc(s_dve_full, 1)
                if kind == "avt":
                    t = ev[2]
                    bank = take_act(ev)
                    pe.wait_ge(s_dve_free, n_dve["vx", b, t])
                    for r in range(RC):
                        last = nc.tensor.transpose(bank[:, tile(r)], avx[:, t % 2, tile(r)], ident[:])
                    last.then_inc(s_act_full, 1)
                if kind == "u":
                    t = ev[2]
                    bank = take_dve(ev)
                    weights("ut", b)
                    pe.wait_ge(s_act_free, n_act["avt", b, t])
                    product(bank[:, 0:D], lambda k: avt[:, t % 2, tile(k)], lambda k: u_t[:, k, :], RC).then_inc(s_dve_full, 1)


def kernel(**inputs):
    import numpy as np
    import concourse.bacc as bacc
    from concourse.bass_utils import run_bass_kernel_spmd

    a = {k: np.asarray(v) for k, v in inputs.items()}
    x = a["L0_attn_X"]
    D = x.shape[-1]
    n = D // P

    def by_pairs(v):
        return v.reshape(-1, HEADS // HPG, 2, n, DH).transpose(0, 3, 1, 2, 4).reshape(v.shape)

    def by_partition(v):
        return v.reshape(n, P).T

    vecs = np.concatenate([by_partition(v) for v in (
        a["L0_attn_ln_g"], a["L0_attn_ln_b"], by_pairs(a["L0_attn_bq"]), by_pairs(a["L0_attn_bk"]), a["L0_ffn_b1"])], axis=1)
    rows = np.concatenate([a["L0_attn_bv"], a["L0_attn_bo"], a["L0_ffn_b2"]])
    ins = {
        "x": x, "vecs": vecs, "rows": rows,
        "wq": by_pairs(a["L0_attn_Wq"]), "wk": by_pairs(a["L0_attn_Wk"]), "wv": a["L0_attn_Wv"], "wo": a["L0_attn_Wo"],
        "w1": a["L0_ffn_W1"], "w2": a["L0_ffn_W2"],
        "vt": a["L0_ffn_V"].transpose(2, 0, 1).reshape(D, -1),
        "ut": a["L0_ffn_U"].transpose(0, 2, 1).reshape(-1, D),
    }
    nc = bacc.Bacc("TRN2", target_bir_lowering=False, num_devices=1)
    arrays, args = {}, []
    for name, v in ins.items():
        v = np.ascontiguousarray(v)
        arrays[f"in_{name}"] = v
        args.append(nc.dram_tensor(f"in_{name}", v.shape, mybir.dt.from_np(v.dtype), kind="ExternalInput").ap())
    out = nc.dram_tensor("out_y", x.shape, mybir.dt.from_np(x.dtype), kind="ExternalOutput").ap()
    block_kernel(nc, *args, out)
    r = run_bass_kernel_spmd(nc, [arrays], core_ids=[0])
    return r.results[0]["out_y"]
```
